# Optimizing a Trainium2 kernel written in Bass

```python
import numpy as np
import jax
import jax.numpy as jnp

def _softmax(x, axis=-1):
    return jax.nn.softmax(x, axis=axis)
def _gelu(x):
    return jax.nn.gelu(x, approximate=True)
def _silu(x):
    return jax.nn.silu(x)
def _sigmoid(x):
    return jax.nn.sigmoid(x)
def _layernorm(x, axis=-1, eps=1e-5):
    m = jnp.mean(x, axis=axis, keepdims=True)
    v = jnp.var(x, axis=axis, keepdims=True)
    return (x - m) / jnp.sqrt(v + eps)
def _scatter_add(tgt, idx, src, axis=0):
    return tgt.at[idx].add(src)
def _segment_sum(src, seg, n):
    return jax.ops.segment_sum(src, seg, n)

kernel_name = 'mk_adj_preln_d2_adj_64_a04720'

def setup_inputs(seed: int = 0):
    np.random.seed(seed)
    _w = jnp.asarray
    def _rec_inputs():
        import jax
        import jax.numpy as jnp
        _gk = jax.random.key(seed)
        x = -0.000929 + 1 * jax.random.normal(jax.random.fold_in(_gk, 1), (8192, 64), jnp.float32)
        _a = jax.random.bernoulli(jax.random.fold_in(_gk, 2), 0.00195312, (8192, 8192))
        _a = jnp.logical_or(_a, jnp.eye(8192, dtype=bool))
        _af = _a.astype(jnp.float32)
        _af = _af * jax.random.uniform(jax.random.fold_in(_gk, 3), (8192, 8192), jnp.float32, 0.05, 1)
        adj = _af
        return x, adj
    x, adj = _rec_inputs()
    def _L0_gnn_setup():
        import jax, jax.numpy as jnp
        import numpy as np
        N = 16384
        F = 64
        O = 64
        key = jax.random.key(seed)
        k1, k2, k3 = jax.random.split(key, 3)
        features = jax.random.normal(k1, (N, F), dtype=jnp.float32)
        adj = jax.random.uniform(k2, (N, N), dtype=jnp.float32)
        W = jax.random.normal(k3, (O, 2 * F), dtype=jnp.float32)
        return {'features': features, 'adj': adj, 'W': W}
    _L0_gnn_all = _L0_gnn_setup()
    _L0_gnn_in = {k: v for k, v in _L0_gnn_all.items() if k in ('W', )}
    del _L0_gnn_all

    def _L1_gnn_setup():
        import jax, jax.numpy as jnp
        import numpy as np
        N, D_IN, D_OUT = (8192, 64, 64)
        MAX_NEIGH = 100
        DECAY = 0.5
        key = jax.random.key(seed)
        k1, k2, k3, k4 = jax.random.split(key, 4)
        stdv = 1.0 / np.sqrt(D_OUT)
        inputs = {'input': jax.random.normal(k1, (N, D_IN), dtype=jnp.float32), 'adj': jax.random.randint(k2, (N, N), 0, 2).astype(jnp.float32), 'weight': jax.random.uniform(k3, (D_IN, D_OUT), minval=-stdv, maxval=stdv, dtype=jnp.float32), 'bias': jax.random.uniform(k4, (D_OUT,), minval=-stdv, maxval=stdv, dtype=jnp.float32)}
        return inputs
    _L1_gnn_all = _L1_gnn_setup()
    _L1_gnn_in = {k: v for k, v in _L1_gnn_all.items() if k in ('weight', 'bias', )}
    del _L1_gnn_all

    return {
        "x": x,
        "adj": adj,
        "L0_gnn_W": _L0_gnn_in["W"],
        "L1_gnn_weight": _L1_gnn_in["weight"],
        "L1_gnn_bias": _L1_gnn_in["bias"],
    }

def reference(x, adj, L0_gnn_W, L1_gnn_weight, L1_gnn_bias):
    import jax
    import jax.numpy as jnp
    def _L0_gnn_ref(features, adj, W):
        import jax, jax.numpy as jnp
        import numpy as np
        N = 16384
        F = 64
        O = 64
        deg = jnp.sum(adj, axis=1, keepdims=True)
        neigh = adj @ features / (deg + 1.0)
        data = jnp.concatenate([features, neigh], axis=-1)
        return data @ W.T

    def _L1_gnn_ref(input, adj, weight, bias):
        import jax, jax.numpy as jnp
        import numpy as np
        N, D_IN, D_OUT = (8192, 64, 64)
        MAX_NEIGH = 100
        DECAY = 0.5
        support = input @ weight
        mask = (adj != 0).astype(support.dtype)
        rank = jnp.cumsum(mask, axis=1)
        deg = rank[:, -1:]
        k = jnp.minimum(deg, float(MAX_NEIGH))
        pos = rank - (deg - k)
        w = mask * jnp.where(pos > 0, DECAY ** (k - pos), 0.0)
        out = w @ support + bias
        return out

    h = jnp.maximum(_layernorm(x, axis=-1), 0.0)
    x = x + _L0_gnn_ref(h, adj, L0_gnn_W)
    h = jnp.maximum(_layernorm(x, axis=-1), 0.0)
    x = x + _L1_gnn_ref(h, adj, L1_gnn_weight, L1_gnn_bias)
    return x


_drawn_inputs = setup_inputs


def setup_inputs(seed=0):
    import zlib

    import numpy as np

    out = dict(_drawn_inputs(seed))
    spreads = {}
    factors = {'L1_gnn_bias': 4.366}
    for name, (base, spread) in spreads.items():
        noise = np.random.default_rng([zlib.crc32(name.encode()), seed]).standard_normal(out[name].shape)
        drawn = base * np.exp(spread * noise) if base else spread * noise
        out[name] = jnp.asarray(drawn.astype(out[name].dtype))
    for name, factor in factors.items():
        out[name] = (out[name] * factor).astype(out[name].dtype)
    return out
```

```python
from contextlib import ExitStack

import concourse.bass as bass
from concourse import mybir

ALU = mybir.AluOpType
ACT = mybir.ActivationFunctionType
AX_X = mybir.AxisListType.X
RMAX = bass.bass_isa.ReduceOp.max
F32 = mybir.dt.float32
BF16 = mybir.dt.bfloat16
F16 = mybir.dt.float16
U8 = mybir.dt.uint8
I16 = mybir.dt.int16

P = 128
F = 64
CHUNK = 512
STRIP = 2 * CHUNK
TILES = STRIP // P
GROUP = 4
SLOTS = 4
MAX_NEIGH = 100
EPS = 1e-5
SUPPORT_SCALE = 512.0
LO_SCALE = 2048.0
CODE_UNIT = 128.0
UNSCALE = 2.0 ** (127 - MAX_NEIGH) / SUPPORT_SCALE
DVE_SHARE = 2560


def build_program(nc, x_t, adj_t, w_t, weight, bias, out_t):
    strips, groups = adj_t.shape[0], adj_t.shape[1]
    tiles = groups * GROUP
    blocks = groups // SLOTS
    assert groups % SLOTS == 0 and blocks >= 2 and strips >= 2 and tiles == strips * TILES
    chunk_tiles = tiles // 4

    codes = nc.dram_tensor("codes", (strips * groups, P, GROUP * STRIP), U8, kind="Internal").ap()
    adj_groups = adj_t.rearrange("s g p c -> (s g) p c")

    with ExitStack() as ctx:
        def sb(name, shape, dt):
            return ctx.enter_context(nc.sbuf_tensor(name, shape, dt))

        def psum(name):
            return ctx.enter_context(nc.psum_tensor(name, [P, CHUNK], F32))

        def sem(name):
            return ctx.enter_context(nc.semaphore(name))

        adj = sb("adj", [P, SLOTS, GROUP * STRIP], F32)
        mask = sb("mask", [P, 2, GROUP, STRIP], BF16)
        code = sb("code", [P, SLOTS, GROUP, STRIP], U8)
        deg_acc = sb("deg_acc", [P, GROUP * STRIP], F32)
        deg_part = sb("deg_part", [P, STRIP], F32)
        x_all = sb("x_all", [P, tiles, F], F32)
        h_all = sb("h_all", [P, tiles, F], F32)
        h_slot = sb("h_slot", [P, SLOTS, GROUP, F], F32)
        h_strip = sb("h_strip", [P, TILES, F], F32)
        support = sb("support", [P, tiles, 2 * F], F16)
        neigh_t = sb("neigh_t", [P, CHUNK], F32)
        feat_t = sb("feat_t", [F, STRIP], F32)
        t_a = sb("t_a", [P, TILES, F], F32)
        t_b = sb("t_b", [P, TILES, F], F32)
        t_c = sb("t_c", [P, TILES, F], F32)
        st = sb("st", [P, 11, 16], F32)
        ident = sb("ident", [P, P], F32)
        ones = sb("ones", [P, 1], F32)
        here = sb("here", [P, P], BF16)
        carry = sb("carry", [P, P], BF16)
        w1 = sb("w1", [F, F], F32)
        w2 = sb("w2", [P, 2, F], F32)
        wn = sb("wn", [F, F], F32)
        merge = sb("merge", [P, F], F32)
        bias_bc = sb("bias_bc", [P, F], F32)
        wm = sb("wm", [P, 8], F32)

        rank_ps = [psum("rank_a"), psum("rank_b")]
        l0_ps = psum("l0")
        deg_ps = psum("deg")
        tr_ps = ctx.enter_context(nc.psum_tensor("tr", [P, 2 * CHUNK], F32))
        agg_ps = psum("agg")
        sup_ps = psum("sup")
        lin_ps = tr_ps[:, 0:CHUNK]

        x_in = [sem(f"x_in{c}") for c in range(4)]
        par_in = sem("par_in")
        adj_in = [sem(f"adj_in{g}") for g in range(SLOTS)]
        h_in = [sem(f"h_in{g}") for g in range(SLOTS)]
        hs_in = sem("hs_in")
        code_out = [sem(f"code_out{g}") for g in range(SLOTS)]
        code_in = [sem(f"code_in{g}") for g in range(SLOTS)]
        out_done = sem("out_done")
        sp_waits = sem("sp_waits")
        pool_chain = sem("pool_chain")
        consts = sem("consts")
        wmax_part = sem("wmax_part")
        wmax_all = sem("wmax_all")
        h_ready = sem("h_ready")
        mask_ready = sem("mask_ready")
        deg_added = sem("deg_added")
        rank_done = sem("rank_done")
        relu_done = sem("relu_done")
        l0_done = sem("l0_done")
        neigh_ready = sem("neigh_ready")
        deg_ready = sem("deg_ready")
        ht_ps = sem("ht_ps")
        agg_done = sem("agg_done")
        ht_ready = sem("ht_ready")
        lin_done = sem("lin_done")
        h1_ready = sem("h1_ready")
        h1t_ps = sem("h1t_ps")
        h1t_ready = sem("h1t_ready")
        sup_done = sem("sup_done")
        hi_done = sem("hi_done")
        res_ready = sem("res_ready")
        lo_done = sem("lo_done")
        var_ready = sem("var_ready")
        std_ready = sem("std_ready")
        dve_step = sem("dve_step")
        dec_dve = sem("dec_dve")
        dec_act = sem("dec_act")
        l1_done = sem("l1_done")
        o_act = sem("o_act")
        o_dve = sem("o_dve")
        fin_ps = sem("fin_ps")
        y_ready = sem("y_ready")

        feat_o = [neigh_t, deg_part[:, 0:CHUNK]]

        def mask_at(g, k):
            return mask[:, g % 2, k, :]

        block = ctx.enter_context(nc.Block())

        @block.sync
        def _(sp):
            def wait(semaphore, count):
                sp.wait_ge(semaphore, count)
                sp.sem_inc(sp_waits, 1)

            for c in (3, 2, 1, 0):
                part = slice(c * chunk_tiles, (c + 1) * chunk_tiles)
                sp.dma_start(x_all[:, part, :], x_t[:, part, :]).then_inc(x_in[c], 16)
                if c == 3:
                    sp.dma_start(adj[:, 0, :], adj_groups[0]).then_inc(adj_in[0], 16)
            sp.dma_start(w1[:], w_t[0:F, :]).then_inc(par_in, 16)
            sp.wait_ge(consts, 1)
            sp.dma_start(w2[0:F, 0, :], w_t[F:2 * F, :]).then_inc(par_in, 16)
            sp.dma_start(w2[F:P, 1, :], w_t[F:2 * F, :]).then_inc(par_in, 16)
            sp.dma_start(wn[:], weight).then_inc(par_in, 16)
            sp.dma_start(bias_bc[:], bias.partition_broadcast(P)).then_inc(par_in, 16)

            def h_tiles(b, g):
                return h_all[:, bass.ds(tiles - GROUP - GROUP * SLOTS * b - GROUP * g, GROUP), :]

            for g in range(SLOTS):
                if g > 0:
                    sp.dma_start(adj[:, g, :], adj_groups[g]).then_inc(adj_in[g], 16)
            for g in range(SLOTS):
                sp.wait_ge(h_ready, 1 + GROUP * (g + 1) // (chunk_tiles + 1))
                sp.dma_start(h_slot[:, g], h_tiles(0, g)).then_inc(h_in[g], 16)
            sp.wait_ge(h_ready, 4)
            sp.dma_start(h_strip[:], h_all[:, 0:TILES, :]).then_inc(hs_in, 16)

            def load_block(s, b):
                for g in range(SLOTS):
                    n = s * groups + b * SLOTS + g
                    wait(mask_ready, n - SLOTS + 1)
                    wait(deg_added, n - SLOTS + 1)
                    wait(l0_done, n - SLOTS + 1)
                    sp.dma_start(adj[:, g, :], adj_groups[n]).then_inc(adj_in[g], 16)
                    sp.dma_start(h_slot[:, g], h_tiles(b, g)).then_inc(h_in[g], 16)
                    wait(relu_done, 2 * GROUP * (n - SLOTS + 1))
                    sp.dma_start(codes[n - SLOTS], code[:, g].rearrange("p k i -> p (k i)")).then_inc(code_out[g], 16)

            with sp.Fori(1, blocks) as b:
                load_block(0, b)
            with sp.Fori(1, strips) as s:
                load_block(s, 0)
                wait(ht_ps, s)
                sp.dma_start(h_strip[:], h_all[:, bass.ds(s * TILES, TILES), :]).then_inc(hs_in, 16)
                with sp.Fori(1, blocks) as b:
                    load_block(s, b)
            total = strips * groups
            for g in range(SLOTS):
                n = total + g
                wait(relu_done, 2 * GROUP * (n - SLOTS + 1))
                sp.dma_start(codes[n - SLOTS], code[:, g].rearrange("p k i -> p (k i)")).then_inc(code_out[g], 16)

            def code_slot(g):
                return adj[:, g, 0:STRIP].bitcast(U8)

            def load_codes(s, b, first):
                for g in range(SLOTS):
                    m = s * groups + b * SLOTS + g
                    if first and g == 0:
                        for q in range(SLOTS):
                            wait(code_out[q], 16 * blocks * (s + 1))
                    wait(dec_dve, m - SLOTS + 1)
                    wait(dec_act, m - SLOTS + 1)
                    sp.dma_start(code_slot(g), codes[s * groups + (groups - 1 - g) - b * SLOTS]).then_inc(code_in[g], 16)

            sp.wait_ge(mask_ready, total)
            sp.wait_ge(deg_added, total)
            sp.wait_ge(l0_done, total)
            for q in range(SLOTS):
                sp.wait_ge(code_out[q], 16 * blocks)
            for g in range(SLOTS):
                sp.dma_start(code_slot(g), codes[groups - 1 - g]).then_inc(code_in[g], 16)
            with sp.Fori(1, blocks) as b:
                load_codes(0, b, False)

            def store_out(s):
                wait(y_ready, s + 1)
                sp.dma_start(out_t[:, bass.ds(s * TILES, TILES), :], t_a[:]).then_inc(out_done, 16)

            with sp.Fori(1, strips) as s:
                load_codes(s, 0, True)
                with sp.Fori(1, blocks) as b:
                    load_codes(s, b, False)
                store_out(s - 1)
            store_out(strips - 1)
            sp.wait_ge(out_done, 16 * strips)
            for q in range(SLOTS):
                sp.wait_ge(code_out[q], 16 * blocks * strips)

        @block.gpsimd
        def _(pool):
            steps = [0]

            def link(ins):
                steps[0] += 1
                ins.then_inc(pool_chain, 1)
                pool.wait_ge(pool_chain, steps[0])

            def diagonal(t, value, base):
                link(nc.gpsimd.affine_select(out=t, in_=t, compare_op=ALU.not_equal, fill=value, base=base,
                                             pattern=[[-1, t.shape[1]]], channel_multiplier=1))

            link(nc.gpsimd.memset(w2[:], 0.0))
            link(nc.gpsimd.memset(ident[:], 0.0))
            diagonal(ident[:], 1.0, 0)
            link(nc.gpsimd.memset(ones[:], 1.0))
            link(nc.gpsimd.memset(here[:], -1.0))
            link(nc.gpsimd.affine_select(out=here[:], in_=here[:], compare_op=ALU.is_gt, fill=0.0, base=0,
                                         pattern=[[-1, P]], channel_multiplier=1))
            diagonal(here[:], float(MAX_NEIGH), 0)
            link(nc.gpsimd.memset(carry[:], -1.0))
            link(nc.gpsimd.affine_select(out=carry[:], in_=carry[:], compare_op=ALU.is_gt, fill=0.0, base=0,
                                         pattern=[[1, P]], channel_multiplier=-1))
            diagonal(carry[:], -1.0 - MAX_NEIGH, 0)
            link(nc.gpsimd.memset(merge[:], 0.0))
            diagonal(merge[:], UNSCALE, 0)
            diagonal(merge[:], UNSCALE / LO_SCALE, -F)
            nc.gpsimd.memset(wm[:], 0.0).then_inc(consts, 1)
            pool.wait_ge(wmax_part, 1)
            nc.gpsimd.partition_all_reduce(wm[:, 3:4], wm[:, 2:3], P, RMAX).then_inc(wmax_all, 1)

        @block.tensor
        def _(pe):
            def rank(s, b, g, k, first, start):
                n = s * groups + b * SLOTS + g
                step = 2 * (GROUP * n + k)
                if k == 0:
                    pe.wait_ge(mask_ready, n + 1)
                for c in range(2):
                    cols = slice(c * CHUNK, (c + 1) * CHUNK)
                    if not (first and start):
                        pe.wait_ge(relu_done, step + c - 1)
                    if not start:
                        prev = mask_at(g, k - 1) if k else mask_at(g + 1, GROUP - 1)
                        nc.tensor.matmul(rank_ps[c][:], carry[:], prev[:, cols], start=False, stop=True,
                                         skip_group_check=True)
                    nc.tensor.matmul(rank_ps[c][:], here[:], mask_at(g, k)[:, cols], start=start, stop=True,
                                     skip_group_check=True).then_inc(rank_done, 1)

            def l0(s, b, g, k, first, start):
                if k == 0:
                    pe.wait_ge(adj_in[g], 16 * (s * blocks + b + 1))
                    pe.wait_ge(h_in[g], 16 * (s * blocks + b + 1))
                if start and not first:
                    pe.wait_ge(neigh_ready, s)
                for c in range(2):
                    cols = slice(k * STRIP + c * CHUNK, k * STRIP + (c + 1) * CHUNK)
                    ins = nc.tensor.matmul(l0_ps[F * c:F * c + F, :], h_slot[:, g, GROUP - 1 - k, :],
                                           adj[:, g, cols], start=start, stop=True, skip_group_check=True)
                if k == GROUP - 1:
                    ins.then_inc(l0_done, 1)

            def end_products(s):
                pe.wait_ge(hs_in, 16 * s)
                for t in range(TILES):
                    ins = nc.tensor.matmul(tr_ps[0:F, t * P:(t + 1) * P], h_strip[:, t, :], ident[:], start=True, stop=True)
                ins.then_inc(ht_ps, 1)
                pe.wait_ge(deg_ready, s)
                for t in range(TILES):
                    nc.tensor.matmul(deg_ps[:, t:t + 1], deg_part[:, t * P:(t + 1) * P], ones[:], start=True, stop=True)
                pe.wait_ge(neigh_ready, s)
                for t in range(TILES):
                    ins = nc.tensor.matmul(agg_ps[:, t * F:(t + 1) * F], neigh_t[:, (t % 4) * P:(t % 4 + 1) * P],
                                           w2[:, t // 4, :], start=True, stop=True)
                ins.then_inc(agg_done, 1)

            def end_linear(s):
                pe.wait_ge(ht_ready, s)
                for t in range(TILES):
                    ins = nc.tensor.matmul(lin_ps[:, t * F:(t + 1) * F], feat_t[:, t * P:(t + 1) * P], w1[:],
                                           start=True, stop=True)
                ins.then_inc(lin_done, 1)

            def end_h1t(s):
                pe.wait_ge(h1_ready, s)
                for t in range(TILES):
                    ins = nc.tensor.matmul(tr_ps[0:F, t * P:(t + 1) * P], t_c[:, t, :], ident[:], start=True, stop=True)
                ins.then_inc(h1t_ps, 1)

            def end_support(s):
                pe.wait_ge(h1t_ready, s)
                for t in range(TILES):
                    ins = nc.tensor.matmul(sup_ps[:, t * F:(t + 1) * F], feat_t[:, t * P:(t + 1) * P], wn[:],
                                           start=True, stop=True)
                ins.then_inc(sup_done, 1)

            end_at = {(0, 1): end_products, (0, 3): end_linear, (2, 1): end_h1t, (2, 3): end_support}

            def sweep_block(s, b, first, start):
                for g in range(SLOTS):
                    for k in range(GROUP):
                        opening = start and g == 0 and k == 0
                        rank(s, b, g, k, first, opening)
                        l0(s, b, g, k, first, opening)
                        if start and not first and (g, k) in end_at:
                            end_at[g, k](s)

            pe.wait_ge(consts, 1)
            pe.wait_ge(par_in, 16 * 5)
            pe.wait_ge(wmax_all, 1)
            sweep_block(0, 0, True, True)
            with pe.Fori(1, blocks) as b:
                sweep_block(0, b, True, False)
            with pe.Fori(1, strips) as s:
                sweep_block(s, 0, False, True)
                with pe.Fori(1, blocks) as b:
                    sweep_block(s, b, False, False)
            for part in (end_products, end_linear, end_h1t, end_support):
                part(strips)

            o_ps = rank_ps

            def product_block(s, b, first, start):
                for g in range(SLOTS):
                    m = s * groups + b * SLOTS + g
                    pe.wait_ge(dec_dve, m + 1)
                    pe.wait_ge(dec_act, m + 1)
                    if start and g == 0 and not first:
                        pe.wait_ge(o_act, s)
                        pe.wait_ge(o_dve, s)
                    w = adj[:, g, 2 * STRIP:4 * STRIP].bitcast(BF16)
                    for k in reversed(range(GROUP)):
                        j = b * (SLOTS * GROUP) + g * GROUP + (GROUP - 1 - k)
                        for c in range(2):
                            ins = nc.tensor.matmul(o_ps[c][:], support[:, bass.ds(j, 1), :].rearrange("p a f -> p (a f)"),
                                                   w[:, k * STRIP + c * CHUNK:k * STRIP + (c + 1) * CHUNK],
                                                   start=start and g == 0 and k == GROUP - 1, stop=True,
                                                   skip_group_check=True)
                    ins.then_inc(l1_done, 1)
                    if start and g == 1 and not first:
                        merge_parts(s)

            def merge_parts(s):
                for t in range(TILES):
                    ins = nc.tensor.matmul(agg_ps[:, t * F:(t + 1) * F], feat_o[t // 4][:, (t % 4) * P:(t % 4 + 1) * P],
                                           merge[:], start=True, stop=True)
                ins.then_inc(fin_ps, 1)

            pe.wait_ge(lo_done, strips)
            product_block(0, 0, True, True)
            with pe.Fori(1, blocks) as b:
                product_block(0, b, True, False)
            with pe.Fori(1, strips) as s:
                product_block(s, 0, False, True)
                with pe.Fori(1, blocks) as b:
                    product_block(s, b, False, False)
            pe.wait_ge(o_act, strips)
            pe.wait_ge(o_dve, strips)
            merge_parts(strips)

        @block.scalar
        def _(act):
            def relu(s, b, g, k):
                n = s * groups + b * SLOTS + g
                step = 2 * (GROUP * n + k)
                for c in range(2):
                    act.wait_ge(rank_done, step + c + 1)
                    nc.scalar.activation(code[:, g, k, c * CHUNK:(c + 1) * CHUNK], rank_ps[c][:], ACT.Relu
                                         ).then_inc(relu_done, 1)

            def neigh_copy(s):
                act.wait_ge(l0_done, s * groups)
                nc.scalar.activation(neigh_t[:], l0_ps[:], ACT.Copy).then_inc(neigh_ready, 1)

            def ht_copy(s):
                act.wait_ge(ht_ps, s)
                nc.scalar.activation(feat_t[:], tr_ps[0:F, :], ACT.Relu).then_inc(ht_ready, 1)

            def h1t_copy(s):
                act.wait_ge(h1t_ps, s)
                nc.scalar.activation(feat_t[:], tr_ps[0:F, :], ACT.Relu).then_inc(h1t_ready, 1)

            def parts_of(s, part):
                return support[:, bass.ds((s - 1) * TILES, TILES), part * F:(part + 1) * F]

            def std(norm, count):
                act.wait_ge(var_ready, norm)
                nc.scalar.activation(st[:, 4, 0:count], st[:, 3, 0:count], ACT.Sqrt).then_inc(std_ready, 1)

            def x1_std(s):
                std(s + 4, TILES)

            def support_hi(s):
                act.wait_ge(sup_done, s)
                nc.scalar.activation(parts_of(s, 0), sup_ps[:].rearrange("p (t f) -> p t f", f=F), ACT.Copy
                                     ).then_inc(hi_done, 1)

            def support_lo(s):
                act.wait_ge(res_ready, s)
                nc.scalar.activation(parts_of(s, 1), t_b[:], ACT.Copy, scale=LO_SCALE).then_inc(lo_done, 1)

            end_at = {(0, 2): ht_copy, (1, 3): x1_std, (2, 2): h1t_copy, (3, 0): support_hi, (3, 2): support_lo}

            def sweep_block(s, b, first, start):
                if start and not first:
                    neigh_copy(s)
                for g in range(SLOTS):
                    if not (first and start):
                        act.wait_ge(code_out[g], 16 * (s * blocks + b))
                    for k in range(GROUP):
                        relu(s, b, g, k)
                        if start and not first and (g, k) in end_at:
                            end_at[g, k](s)

            for c in range(4):
                std(c + 1, chunk_tiles)
            sweep_block(0, 0, True, True)
            with act.Fori(1, blocks) as b:
                sweep_block(0, b, True, False)
            with act.Fori(1, strips) as s:
                sweep_block(s, 0, False, True)
                with act.Fori(1, blocks) as b:
                    sweep_block(s, b, False, False)
            for part in (neigh_copy, ht_copy, x1_std, h1t_copy, support_hi, support_lo):
                part(strips)

            def sums_out(s):
                act.wait_ge(l1_done, s * groups)
                nc.scalar.activation(feat_o[0][:], rank_ps[0][:], ACT.Copy).then_inc(o_act, 1)

            def decode_block(s, b, first, start):
                for g in range(SLOTS):
                    m = s * groups + b * SLOTS + g
                    act.wait_ge(code_in[g], 16 * (s * blocks + b + 1))
                    if not (first and start):
                        act.wait_ge(l1_done, m - SLOTS + 1)
                    cols = slice(DVE_SHARE, GROUP * STRIP)
                    nc.scalar.activation(adj[:, g, 2 * STRIP:4 * STRIP].bitcast(I16)[:, cols],
                                         adj[:, g, 0:STRIP].bitcast(U8)[:, cols], ACT.Copy, scale=CODE_UNIT
                                         ).then_inc(dec_act, 1)
                    if start and g == 2 and not first:
                        sums_out(s)

            decode_block(0, 0, True, True)
            with act.Fori(1, blocks) as b:
                decode_block(0, b, True, False)
            with act.Fori(1, strips) as s:
                decode_block(s, 0, False, True)
                with act.Fori(1, blocks) as b:
                    decode_block(s, b, False, False)
            sums_out(strips)

        @block.vector
        def _(dve):
            def per_tile(col, count=TILES):
                return st[:, col, 0:count].unsqueeze(2).to_broadcast([P, count, F])

            LN_STEPS = 9

            def layernorm(src, centred, squares, result, count, done, norm):
                nc.vector.tensor_reduce(st[:, 0, 0:count], src, AX_X, ALU.add).then_inc(dve_step, 1)
                dve.wait_ge(dve_step, done + 1)
                nc.vector.tensor_scalar(st[:, 1, 0:count], st[:, 0, 0:count], 1.0 / F, None, ALU.mult).then_inc(dve_step, 1)
                dve.wait_ge(dve_step, done + 2)
                nc.vector.tensor_tensor(centred, src, per_tile(1, count), ALU.subtract).then_inc(dve_step, 1)
                dve.wait_ge(dve_step, done + 3)
                nc.vector.tensor_tensor(squares, centred, centred, ALU.mult).then_inc(dve_step, 1)
                dve.wait_ge(dve_step, done + 4)
                nc.vector.tensor_reduce(st[:, 2, 0:count], squares, AX_X, ALU.add).then_inc(dve_step, 1)
                dve.wait_ge(dve_step, done + 5)
                nc.vector.tensor_scalar(st[:, 3, 0:count], st[:, 2, 0:count], 1.0 / F, EPS, ALU.mult, ALU.add
                                        ).then_inc(var_ready, 1)
                dve.wait_ge(std_ready, norm)
                nc.vector.reciprocal(st[:, 5, 0:count], st[:, 4, 0:count]).then_inc(dve_step, 1)
                dve.wait_ge(dve_step, done + 6)
                nc.vector.scalar_tensor_tensor(st[:, 6, 0:count], st[:, 3, 0:count], -0.5, st[:, 5, 0:count],
                                               ALU.mult, ALU.mult).then_inc(dve_step, 1)
                dve.wait_ge(dve_step, done + 7)
                nc.vector.tensor_tensor(st[:, 7, 0:count], st[:, 6, 0:count], st[:, 5, 0:count], ALU.mult
                                        ).then_inc(dve_step, 1)
                dve.wait_ge(dve_step, done + 8)
                nc.vector.scalar_tensor_tensor(st[:, 8, 0:count], st[:, 7, 0:count], 1.5, st[:, 5, 0:count],
                                               ALU.add, ALU.mult).then_inc(dve_step, 1)
                dve.wait_ge(dve_step, done + 9)
                return nc.vector.tensor_tensor(result, centred, per_tile(8, count), ALU.mult)

            quarter = chunk_tiles * F
            done = 0
            for c in (3, 2, 1, 0):
                part = slice(c * chunk_tiles, (c + 1) * chunk_tiles)
                tmp = [deg_acc[:, q * quarter:(q + 1) * quarter].rearrange("p (t f) -> p t f", f=F) for q in range(3)]
                dve.wait_ge(x_in[c], 16)
                layernorm(x_all[:, part, :], tmp[0], tmp[1], tmp[2], chunk_tiles, done, 4 - c).then_inc(dve_step, 1)
                done += LN_STEPS + 1
                dve.wait_ge(dve_step, done)
                nc.vector.tensor_scalar(h_all[:, part, :], tmp[2], 0.0, None, ALU.max).then_inc(h_ready, 1)

            dve.wait_ge(consts, 1)
            dve.wait_ge(par_in, 16 * 5)
            nc.vector.tensor_reduce(wm[0:F, 0:1], wn[:], AX_X, ALU.max).then_inc(dve_step, 1)
            nc.vector.tensor_reduce(wm[0:F, 1:2], wn[:], AX_X, ALU.min).then_inc(dve_step, 1)
            done += 2
            dve.wait_ge(dve_step, done)
            nc.vector.scalar_tensor_tensor(wm[0:F, 2:3], wm[0:F, 1:2], -1.0, wm[0:F, 0:1], ALU.mult, ALU.max
                                           ).then_inc(wmax_part, 1)
            dve.wait_ge(wmax_all, 1)
            nc.vector.tensor_scalar(wm[:, 4:5], wm[:, 3:4], 1e-30, None, ALU.max).then_inc(dve_step, 1)
            done += 1
            dve.wait_ge(dve_step, done)
            nc.vector.reciprocal(wm[:, 5:6], wm[:, 4:5]).then_inc(dve_step, 1)
            done += 1
            dve.wait_ge(dve_step, done)
            nc.vector.tensor_scalar(wn[:], wn[:], wm[0:F, 5:6], SUPPORT_SCALE, ALU.mult, ALU.mult).then_inc(dve_step, 1)
            nc.vector.tensor_scalar(merge[:], merge[:], wm[:, 4:5], None, ALU.mult).then_inc(dve_step, 1)
            done += 2
            dve.wait_ge(dve_step, done)
            setup_done = done

            END_STEPS = 6 + LN_STEPS + 1

            def masks(s, b, g, first, start):
                n = s * groups + b * SLOTS + g
                dve.wait_ge(adj_in[g], 16 * (s * blocks + b + 1))
                if not (first and start and g < 2):
                    dve.wait_ge(rank_done, 2 * GROUP * (n - 1) + 2)
                nc.vector.tensor_scalar(mask[:, g % 2].rearrange("p k i -> p (k i)"), adj[:, g, :], 0.0, None,
                                        ALU.not_equal).then_inc(mask_ready, 1)

            def row_sums(s, b, g, first, start):
                n = s * groups + b * SLOTS + g
                if start and g == 0:
                    if not first:
                        dve.wait_ge(deg_ready, s)
                    nc.vector.tensor_copy(deg_acc[:], adj[:, g, :]).then_inc(deg_added, 1)
                else:
                    dve.wait_ge(deg_added, n)
                    nc.vector.tensor_tensor(deg_acc[:], deg_acc[:], adj[:, g, :], ALU.add).then_inc(deg_added, 1)

            def base(s):
                return setup_done + (s - 1) * END_STEPS

            def fold(s):
                dve.wait_ge(deg_added, s * groups)
                half = GROUP * STRIP // 2
                nc.vector.tensor_tensor(deg_acc[:, 0:half], deg_acc[:, 0:half], deg_acc[:, half:], ALU.add
                                        ).then_inc(dve_step, 1)
                dve.wait_ge(dve_step, base(s) + 1)
                nc.vector.tensor_tensor(deg_part[:], deg_acc[:, 0:STRIP], deg_acc[:, STRIP:half], ALU.add
                                        ).then_inc(deg_ready, 1)

            def new_x(s):
                own = x_all[:, bass.ds((s - 1) * TILES, TILES), :]
                at = base(s)
                dve.wait_ge(lin_done, s)
                nc.vector.tensor_scalar(st[:, 9, 0:TILES], deg_ps[:, 0:TILES], 1.0, None, ALU.add).then_inc(dve_step, 1)
                dve.wait_ge(dve_step, at + 2)
                nc.vector.reciprocal(st[:, 10, 0:TILES], st[:, 9, 0:TILES]).then_inc(dve_step, 1)
                dve.wait_ge(dve_step, at + 3)
                nc.vector.tensor_tensor(t_a[:], agg_ps[:].rearrange("p (t f) -> p t f", f=F), per_tile(10), ALU.mult
                                        ).then_inc(dve_step, 1)
                dve.wait_ge(dve_step, at + 4)
                nc.vector.tensor_tensor(t_b[:], t_a[:], lin_ps.rearrange("p (t f) -> p t f", f=F), ALU.add
                                        ).then_inc(dve_step, 1)
                dve.wait_ge(dve_step, at + 5)
                nc.vector.tensor_tensor(t_a[:], t_b[:], own, ALU.add).then_inc(dve_step, 1)
                dve.wait_ge(dve_step, at + 6)
                layernorm(t_a[:], t_b[:], t_c[:], t_c[:], TILES, at + 6, s + 4).then_inc(h1_ready, 1)
                nc.vector.tensor_tensor(own, t_a[:], bias_bc[:].unsqueeze(1).to_broadcast([P, TILES, F]), ALU.add
                                        ).then_inc(dve_step, 1)

            def residue(s):
                dve.wait_ge(hi_done, s)
                nc.vector.tensor_tensor(t_b[:], sup_ps[:].rearrange("p (t f) -> p t f", f=F),
                                        support[:, bass.ds((s - 1) * TILES, TILES), 0:F], ALU.subtract
                                        ).then_inc(res_ready, 1)

            def sweep_block(s, b, first, start):
                end = start and not first
                for g in range(SLOTS):
                    masks(s, b, g, first, start)
                    if end and g == 0:
                        fold(s)
                    row_sums(s, b, g, first, start)
                    if end and g == 1:
                        new_x(s)
                    if end and g == 3:
                        residue(s)

            sweep_block(0, 0, True, True)
            with dve.Fori(1, blocks) as b:
                sweep_block(0, b, True, False)
            with dve.Fori(1, strips) as s:
                sweep_block(s, 0, False, True)
                with dve.Fori(1, blocks) as b:
                    sweep_block(s, b, False, False)
            fold(strips)
            new_x(strips)
            residue(strips)

            def sums_out(s):
                dve.wait_ge(l1_done, s * groups)
                nc.vector.tensor_copy(feat_o[1], rank_ps[1][:]).then_inc(o_dve, 1)

            def result(s, last):
                dve.wait_ge(fin_ps, s)
                nc.vector.tensor_tensor(t_a[:], agg_ps[:].rearrange("p (t f) -> p t f", f=F),
                                        x_all[:, bass.ds((s - 1) * TILES, TILES), :], ALU.add).then_inc(y_ready, 1)

            def decode_block(s, b, first, start):
                for g in range(SLOTS):
                    m = s * groups + b * SLOTS + g
                    dve.wait_ge(code_in[g], 16 * (s * blocks + b + 1))
                    if not (first and start):
                        dve.wait_ge(l1_done, m - SLOTS + 1)
                    cols = slice(0, DVE_SHARE)
                    nc.vector.tensor_scalar(adj[:, g, 2 * STRIP:4 * STRIP].bitcast(I16)[:, cols],
                                            adj[:, g, 0:STRIP].bitcast(U8)[:, cols], CODE_UNIT, None, ALU.mult
                                            ).then_inc(dec_dve, 1)
                    if start and g == 2 and not first:
                        sums_out(s)
                if start and not first:
                    result(s, False)

            decode_block(0, 0, True, True)
            with dve.Fori(1, blocks) as b:
                decode_block(0, b, True, False)
            with dve.Fori(1, strips) as s:
                decode_block(s, 0, False, True)
                with dve.Fori(1, blocks) as b:
                    decode_block(s, b, False, False)
                dve.wait_ge(out_done, 16 * s)
            sums_out(strips)
            result(strips, True)


def kernel(x, adj, L0_gnn_W, L1_gnn_weight, L1_gnn_bias):
    import numpy as np
    import concourse.bacc as bacc
    from concourse.bass_utils import run_bass_kernel_spmd

    x, adj = np.asarray(x), np.asarray(adj)
    n = x.shape[0]
    strips, tiles = n // STRIP, n // P
    adj_t = adj.reshape(strips, STRIP, tiles // GROUP, GROUP, P)[:, :, ::-1, ::-1, :]
    arrays = {
        "x_t": np.ascontiguousarray(x.reshape(tiles, P, F).transpose(1, 0, 2)),
        "adj_t": np.ascontiguousarray(adj_t.transpose(0, 2, 4, 3, 1)).reshape(strips, tiles // GROUP, P, GROUP * STRIP),
        "w_t": np.ascontiguousarray(np.asarray(L0_gnn_W).T),
        "weight": np.ascontiguousarray(L1_gnn_weight),
        "bias": np.ascontiguousarray(L1_gnn_bias),
    }
    nc = bacc.Bacc("TRN2", target_bir_lowering=False, num_devices=1)
    args = [nc.dram_tensor(k, a.shape, mybir.dt.from_np(a.dtype), kind="ExternalInput").ap() for k, a in arrays.items()]
    args.append(nc.dram_tensor("out_t", (P, tiles, F), F32, kind="ExternalOutput").ap())
    build_program(nc, *args)
    result = run_bass_kernel_spmd(nc, [arrays], core_ids=[0])
    return np.ascontiguousarray(result.results[0]["out_t"].transpose(1, 0, 2)).reshape(n, F)
```

```python
from contextlib import ExitStack

import concourse.bass as bass
from concourse import mybir

ALU = mybir.AluOpType
ACT = mybir.ActivationFunctionType
AX_X = mybir.AxisListType.X
RMAX = bass.bass_isa.ReduceOp.max
F32 = mybir.dt.float32
BF16 = mybir.dt.bfloat16
F16 = mybir.dt.float16
U8 = mybir.dt.uint8
I16 = mybir.dt.int16

P = 128
F = 64
CHUNK = 512
STRIP = 2 * CHUNK
TILES = STRIP // P
GROUP = 4
SLOTS = 4
MAX_NEIGH = 100
EPS = 1e-5
SUPPORT_SCALE = 512.0
LO_SCALE = 2048.0
CODE_UNIT = 128.0
UNSCALE = 2.0 ** (127 - MAX_NEIGH) / SUPPORT_SCALE
DVE_SHARE = 2560


def build_program(nc, x_t, adj_t, w_t, weight, bias, out_t):
    strips, groups = adj_t.shape[0], adj_t.shape[1]
    tiles = groups * GROUP
    blocks = groups // SLOTS
    assert groups % SLOTS == 0 and blocks >= 2 and strips >= 2 and tiles == strips * TILES
    chunk_tiles = tiles // 4

    def direct_blocks(s):
        return min(blocks - 1, s * TILES // (GROUP * SLOTS))

    runs = []
    for s in range(strips):
        if s > 1 and direct_blocks(s) == runs[-1][2]:
            runs[-1][1] = s + 1
        else:
            runs.append([s, s + 1, direct_blocks(s), sum(blocks - direct_blocks(q) for q in range(s)),
                         sum(direct_blocks(q) for q in range(s))])
    stored_total = sum(blocks - direct_blocks(s) for s in range(strips))
    direct_total = sum(direct_blocks(s) for s in range(strips))
    BLOCK_TILES = GROUP * SLOTS

    def loop(engine, first, end, body):
        if end - first == 1:
            body(first)
        elif end > first:
            with engine.Fori(first, end) as i:
                body(i)

    codes = nc.dram_tensor("codes", (strips * groups, P, GROUP * STRIP), U8, kind="Internal").ap()
    adj_groups = adj_t.rearrange("s g p c -> (s g) p c")

    with ExitStack() as ctx:
        def sb(name, shape, dt):
            return ctx.enter_context(nc.sbuf_tensor(name, shape, dt))

        def psum(name):
            return ctx.enter_context(nc.psum_tensor(name, [P, CHUNK], F32))

        def sem(name):
            return ctx.enter_context(nc.semaphore(name))

        adj = sb("adj", [P, SLOTS, GROUP * STRIP], F32)
        mask = sb("mask", [P, 2, GROUP, STRIP], BF16)
        code = sb("code", [P, SLOTS, GROUP, STRIP], U8)
        deg_acc = sb("deg_acc", [P, GROUP * STRIP], F32)
        deg_part = sb("deg_part", [P, STRIP], F32)
        x_all = sb("x_all", [P, tiles, F], F32)
        h_wrap = sb("h_wrap", [P, GROUP + tiles, F], F32)
        h_all = h_wrap[:, GROUP:, :]
        h_slot = sb("h_slot", [P, SLOTS, GROUP, F], F32)
        h_strip = sb("h_strip", [P, TILES, F], F32)
        support = sb("support", [P, tiles, 2 * F], F16)
        neigh_t = sb("neigh_t", [P, CHUNK], F32)
        feat_t = sb("feat_t", [P, CHUNK], F32)
        w_direct = sb("w_direct", [P, 2, STRIP], BF16)
        partial_t = sb("partial_t", [P, STRIP], F32)
        t_a = sb("t_a", [P, TILES, F], F32)
        t_b = sb("t_b", [P, TILES, F], F32)
        t_c = sb("t_c", [P, TILES, F], F32)
        st = sb("st", [P, 11, 16], F32)
        ident = sb("ident", [P, P], F32)
        ones = sb("ones", [P, 1], F32)
        here = sb("here", [P, P], BF16)
        carry = sb("carry", [P, P], BF16)
        zeros = sb("zeros", [P, CHUNK], BF16)
        w1 = sb("w1", [P, 2, F], F32)
        w2 = sb("w2", [P, 2, F], F32)
        wn = sb("wn", [P, 2, F], F32)
        merge = sb("merge", [P, F], F32)
        bias_bc = sb("bias_bc", [P, F], F32)
        wm = sb("wm", [P, 8], F32)

        rank_ps = [psum("rank_a"), psum("rank_b")]
        l0_ps = psum("l0")
        tr_ps = psum("tr")
        agg_ps = psum("agg")
        sup_ps = psum("sup")
        part_ps = ctx.enter_context(nc.psum_tensor("part", [P, STRIP], F32))
        lin_ps = tr_ps[:]
        deg_ps = sup_ps[:, 0:TILES]

        x_in = [sem(f"x_in{c}") for c in range(4)]
        par_in = sem("par_in")
        adj_in = [sem(f"adj_in{g}") for g in range(SLOTS)]
        hs_in = sem("hs_in")
        code_out = [sem(f"code_out{g}") for g in range(SLOTS)]
        code_in = [sem(f"code_in{g}") for g in range(SLOTS)]
        out_done = sem("out_done")
        sp_waits = sem("sp_waits")
        pool_chain = sem("pool_chain")
        consts = sem("consts")
        wmax_part = sem("wmax_part")
        wmax_all = sem("wmax_all")
        h_ready = sem("h_ready")
        mask_ready = sem("mask_ready")
        deg_added = sem("deg_added")
        h_moved = sem("h_moved")
        rank_done = sem("rank_done")
        part_used = sem("part_used")
        relu_done = sem("relu_done")
        l0_done = sem("l0_done")
        neigh_ready = sem("neigh_ready")
        deg_ready = sem("deg_ready")
        ht_ps = sem("ht_ps")
        agg_done = sem("agg_done")
        ht_ready = sem("ht_ready")
        lin_done = sem("lin_done")
        h1_ready = sem("h1_ready")
        h1t_ps = sem("h1t_ps")
        h1t_ready = sem("h1t_ready")
        sup_done = sem("sup_done")
        hi_done = sem("hi_done")
        res_ready = sem("res_ready")
        lo_done = sem("lo_done")
        part_ready = sem("part_ready")
        part_done = sem("part_done")
        var_ready = sem("var_ready")
        std_ready = sem("std_ready")
        own_done = sem("own_done")
        dve_step = sem("dve_step")
        dec_dve = sem("dec_dve")
        dec_act = sem("dec_act")
        l1_done = sem("l1_done")
        o_act = sem("o_act")
        o_dve = sem("o_dve")
        fin_ps = sem("fin_ps")
        y_ready = sem("y_ready")

        feat_o = [neigh_t, deg_part[:, 0:CHUNK]]

        def mask_at(g, k):
            return mask[:, g % 2, k, :]

        block = ctx.enter_context(nc.Block())

        @block.sync
        def _(sp):
            def wait(semaphore, count):
                sp.wait_ge(semaphore, count)
                sp.sem_inc(sp_waits, 1)

            for c in (3, 2, 1, 0):
                part = slice(c * chunk_tiles, (c + 1) * chunk_tiles)
                sp.dma_start(x_all[:, part, :], x_t[:, part, :]).then_inc(x_in[c], 16)
                if c > 1:
                    sp.dma_start(adj[:, 3 - c, :], adj_groups[3 - c]).then_inc(adj_in[3 - c], 16)
            for g in range(2, SLOTS):
                sp.dma_start(adj[:, g, :], adj_groups[g]).then_inc(adj_in[g], 16)
            sp.wait_ge(consts, 1)
            for half in range(2):
                rows = slice(half * F, half * F + F)
                sp.dma_start(w1[rows, half, :], w_t[0:F, :]).then_inc(par_in, 16)
                sp.dma_start(w2[rows, half, :], w_t[F:2 * F, :]).then_inc(par_in, 16)
                sp.dma_start(wn[rows, half, :], weight).then_inc(par_in, 16)
            sp.dma_start(bias_bc[:], bias.partition_broadcast(P)).then_inc(par_in, 16)
            sp.wait_ge(h_ready, 4)
            sp.dma_start(h_strip[:], h_all[:, 0:TILES, :]).then_inc(hs_in, 16)

            def load_block(s, b):
                for g in range(SLOTS):
                    n = s * groups + b * SLOTS + g
                    wait(mask_ready, n - SLOTS + 1)
                    wait(deg_added, n - SLOTS + 1)
                    wait(l0_done, n - SLOTS + 1)
                    sp.dma_start(adj[:, g, :], adj_groups[n]).then_inc(adj_in[g], 16)

            loop(sp, 1, blocks, lambda b: load_block(0, b))
            with sp.Fori(1, strips) as s:
                load_block(s, 0)
                wait(ht_ps, s)
                sp.dma_start(h_strip[:], h_all[:, bass.ds(s * TILES, TILES), :]).then_inc(hs_in, 16)
                loop(sp, 1, blocks, lambda b: load_block(s, b))

            total = strips * groups

            def load_codes(s, b, stored, before, prefetch):
                for g in range(SLOTS):
                    m = (before + b) * SLOTS + g
                    if prefetch:
                        last = total - SLOTS + g + 1
                        sp.wait_ge(mask_ready, last)
                        sp.wait_ge(deg_added, last)
                        sp.wait_ge(l0_done, last)
                    else:
                        wait(dec_dve, m - SLOTS + 1)
                        if not isinstance(m, int) or m >= 2 * SLOTS:
                            wait(dec_act, m + 1 - 2 * SLOTS)
                    sp.dma_start(adj[:, g, 0:STRIP].bitcast(U8), codes[s * groups + (stored * SLOTS - 1 - g) - b * SLOTS]
                                 ).then_inc(code_in[g], 16)

            def store_out(s):
                wait(y_ready, s + 1)
                sp.dma_start(out_t[:, bass.ds(s * TILES, TILES), :], t_a[:]).then_inc(out_done, 16)

            for q in range(SLOTS):
                sp.wait_ge(code_out[q], 16 * blocks)
            load_codes(0, 0, blocks, 0, True)
            load_codes(0, 1, blocks, 0, False)
            loop(sp, 2, blocks, lambda b: load_codes(0, b, blocks, 0, False))
            for q in range(SLOTS):
                sp.wait_ge(code_out[q], 16 * stored_total)
            for s0, s1, direct, stored0, _ in runs[1:]:
                stored = blocks - direct

                def codes_of(s):
                    before = (s - s0) * stored + stored0
                    load_codes(s, 0, stored, before, False)
                    loop(sp, 1, stored, lambda b: load_codes(s, b, stored, before, False))
                    store_out(s - 1)

                loop(sp, s0, s1, codes_of)
            store_out(strips - 1)
            sp.wait_ge(out_done, 16 * strips)

        @block.gpsimd
        def _(pool):
            steps = [0]

            def link(ins):
                steps[0] += 1
                ins.then_inc(pool_chain, 1)
                pool.wait_ge(pool_chain, steps[0])

            def diagonal(t, value, base):
                link(nc.gpsimd.affine_select(out=t, in_=t, compare_op=ALU.not_equal, fill=value, base=base,
                                             pattern=[[-1, t.shape[1]]], channel_multiplier=1))

            link(nc.gpsimd.memset(here[:], -1.0))
            link(nc.gpsimd.affine_select(out=here[:], in_=here[:], compare_op=ALU.is_gt, fill=0.0, base=0,
                                         pattern=[[-1, P]], channel_multiplier=1))
            diagonal(here[:], float(MAX_NEIGH), 0)
            link(nc.gpsimd.memset(carry[:], -1.0))
            link(nc.gpsimd.affine_select(out=carry[:], in_=carry[:], compare_op=ALU.is_gt, fill=0.0, base=0,
                                         pattern=[[1, P]], channel_multiplier=-1))
            diagonal(carry[:], -1.0 - MAX_NEIGH, 0)
            for matrix in (zeros, w1, w2, wn, ident):
                link(nc.gpsimd.memset(matrix[:], 0.0))
            diagonal(ident[:], 1.0, 0)
            link(nc.gpsimd.memset(ones[:], 1.0))
            link(nc.gpsimd.memset(merge[:], 0.0))
            diagonal(merge[:], UNSCALE, 0)
            diagonal(merge[:], UNSCALE / LO_SCALE, -F)
            nc.gpsimd.nop().then_inc(consts, 1)
            pool.wait_ge(wmax_part, 1)
            nc.gpsimd.partition_all_reduce(wm[:, 3:4], wm[:, 2:3], P, RMAX).then_inc(wmax_all, 1)

        @block.tensor
        def _(pe):
            def rank(s, b, g, k, first, start):
                n = s * groups + b * SLOTS + g
                step = 2 * (GROUP * n + k)
                if k == 0:
                    pe.wait_ge(mask_ready, n + 1)
                for c in range(2):
                    cols = slice(c * CHUNK, (c + 1) * CHUNK)
                    if not (first and start):
                        pe.wait_ge(relu_done, step + c - 1)
                    if not start:
                        prev = mask_at(g, k - 1) if k else mask_at(g + 1, GROUP - 1)
                        nc.tensor.matmul(rank_ps[c][:], carry[:], prev[:, cols], start=False, stop=True,
                                         skip_group_check=True)
                    nc.tensor.matmul(rank_ps[c][:], here[:], mask_at(g, k)[:, cols], start=start, stop=True,
                                     skip_group_check=True).then_inc(rank_done, 1)

            def l0(s, b, g, k, first, start):
                n = s * groups + b * SLOTS + g
                if k == 0:
                    pe.wait_ge(adj_in[g], 16 * (s * blocks + b + 1))
                    pe.wait_ge(h_moved, n + 1)
                if start and not first:
                    pe.wait_ge(neigh_ready, s)
                for c in range(2):
                    cols = slice(k * STRIP + c * CHUNK, k * STRIP + (c + 1) * CHUNK)
                    ins = nc.tensor.matmul(l0_ps[F * c:F * c + F, :], h_slot[:, g, GROUP - 1 - k, :],
                                           adj[:, g, cols], start=start, stop=True, skip_group_check=True)
                if k == GROUP - 1:
                    ins.then_inc(l0_done, 1)

            def half_of(t):
                return slice(F * (t // 4), F * (t // 4) + F)

            def in_half(t):
                return slice((t % 4) * P, (t % 4 + 1) * P)

            def end_products(s):
                pe.wait_ge(hs_in, 16 * s)
                for t in range(TILES):
                    ins = nc.tensor.matmul(tr_ps[half_of(t), in_half(t)], h_strip[:, t, :], ident[:], start=True, stop=True)
                ins.then_inc(ht_ps, 1)
                pe.wait_ge(neigh_ready, s)
                for t in range(TILES):
                    ins = nc.tensor.matmul(agg_ps[:, t * F:(t + 1) * F], neigh_t[:, in_half(t)],
                                           w2[:, t // 4, :], start=True, stop=True)
                ins.then_inc(agg_done, 1)

            def end_linear(s):
                pe.wait_ge(deg_ready, s)
                if not isinstance(s, int) or s > 1:
                    pe.wait_ge(res_ready, s - 1)
                for t in range(TILES):
                    nc.tensor.matmul(deg_ps[:, t:t + 1], deg_part[:, t * P:(t + 1) * P], ones[:], start=True, stop=True)
                pe.wait_ge(ht_ready, s)
                for t in range(TILES):
                    ins = nc.tensor.matmul(lin_ps[:, t * F:(t + 1) * F], feat_t[:, in_half(t)], w1[:, t // 4, :],
                                           start=True, stop=True)
                ins.then_inc(lin_done, 1)

            def end_h1t(s):
                pe.wait_ge(h1_ready, s)
                for t in range(TILES):
                    ins = nc.tensor.matmul(tr_ps[half_of(t), in_half(t)], t_c[:, t, :], ident[:], start=True, stop=True)
                ins.then_inc(h1t_ps, 1)

            def end_support(s):
                pe.wait_ge(h1t_ready, s)
                for t in range(TILES):
                    ins = nc.tensor.matmul(sup_ps[:, t * F:(t + 1) * F], feat_t[:, in_half(t)], wn[:, t // 4, :],
                                           start=True, stop=True)
                ins.then_inc(sup_done, 1)

            def end_partial(s):
                pe.wait_ge(part_ready, s)
                for t in range(TILES):
                    ins = nc.tensor.matmul(tr_ps[:, t * F:(t + 1) * F], partial_t[:, t * P:(t + 1) * P], merge[:],
                                           start=True, stop=True)
                ins.then_inc(part_done, 1)

            end_at = {(0, 0): [end_products], (0, 2): [end_linear], (2, 1): [end_h1t], (2, 3): [end_support, end_partial]}

            def open_sums(s):
                if not isinstance(s, int) or s > 0:
                    pe.wait_ge(part_ready, s)
                for c in range(2):
                    nc.tensor.matmul(part_ps[:, c * CHUNK:(c + 1) * CHUNK], zeros[:, 0:P], zeros[:],
                                     start=True, stop=True, skip_group_check=True).then_inc(part_used, 1)

            def l1_direct(s, b, g, k):
                step = 2 * (GROUP * (s * groups + b * SLOTS + g) + k)
                parts = support_of(b * -BLOCK_TILES + (tiles - 1 - g * GROUP - k))
                for c in range(2):
                    cols = slice(c * CHUNK, (c + 1) * CHUNK)
                    pe.wait_ge(relu_done, step + c + 1)
                    ins = nc.tensor.matmul(part_ps[:, cols], parts, w_direct[:, k % 2, cols],
                                           start=False, stop=True, skip_group_check=True)
                ins.then_inc(part_used, 1)

            def support_of(tile):
                return support[:, bass.ds(tile, 1), :].rearrange("p a f -> p (a f)")

            def sweep_block(s, b, first, start, direct=False):
                for g in range(SLOTS):
                    for k in range(GROUP):
                        opening = start and g == 0 and k == 0
                        rank(s, b, g, k, first, opening)
                        l0(s, b, g, k, first, opening)
                        if direct:
                            l1_direct(s, b, g, k)
                        if start and not first:
                            for part in end_at.get((g, k), []):
                                part(s)

            pe.wait_ge(consts, 1)
            for s0, s1, direct, _, _ in runs:

                def strip(s):
                    first = s0 == 0
                    sweep_block(s, 0, first, True)
                    loop(pe, 1, blocks - direct, lambda b: sweep_block(s, b, first, False))
                    if direct:
                        pe.wait_ge(lo_done, s)
                    open_sums(s)
                    loop(pe, blocks - direct, blocks, lambda b: sweep_block(s, b, False, False, True))

                loop(pe, s0, s1, strip)
                if s0 == 0:
                    pe.wait_ge(par_in, 16 * 7)

            o_ps = rank_ps
            end_late = {0: [end_linear], 6: [end_h1t], 8: [end_support, end_partial]}

            def product_group(s, b, g, stored, before, start):
                m = (before + b) * SLOTS + g
                pe.wait_ge(dec_dve, m + 1)
                if not isinstance(m, int) or m >= SLOTS:
                    pe.wait_ge(dec_act, m + 1 - SLOTS)
                w = adj[:, g, 2 * STRIP:4 * STRIP].bitcast(BF16)
                for k in reversed(range(GROUP)):
                    tile = b * BLOCK_TILES + (tiles - stored * BLOCK_TILES + g * GROUP + (GROUP - 1 - k))
                    for c in range(2):
                        ins = nc.tensor.matmul(o_ps[c][:], support_of(tile),
                                               w[:, k * STRIP + c * CHUNK:k * STRIP + (c + 1) * CHUNK],
                                               start=start and g == 0 and k == GROUP - 1, stop=True,
                                               skip_group_check=True)
                ins.then_inc(l1_done, 1)

            def product_block(s, b, stored, before, start):
                if start:
                    pe.wait_ge(o_act, s)
                    pe.wait_ge(o_dve, s)
                for g in range(SLOTS):
                    product_group(s, b, g, stored, before, start)
                    if start and g == 1:
                        merge_parts(s)

            def merge_parts(s):
                for t in range(TILES):
                    ins = nc.tensor.matmul(agg_ps[:, t * F:(t + 1) * F], feat_o[t // 4][:, (t % 4) * P:(t % 4 + 1) * P],
                                           merge[:], start=True, stop=True)
                ins.then_inc(fin_ps, 1)

            pe.wait_ge(relu_done, 2 * tiles * strips)
            pe.wait_ge(lo_done, strips - 1)
            end_products(strips)
            for m in range(groups):
                if m == groups - TILES // GROUP:
                    pe.wait_ge(lo_done, strips)
                product_group(0, m // SLOTS, m % SLOTS, blocks, 0, m == 0)
                for part in end_late.get(m, []):
                    part(strips)
            for s0, s1, direct, stored0, _ in runs[1:]:
                stored = blocks - direct

                def product_strip(s):
                    before = (s - s0) * stored + stored0
                    product_block(s, 0, stored, before, True)
                    loop(pe, 1, stored, lambda b: product_block(s, b, stored, before, False))

                loop(pe, s0, s1, product_strip)
            pe.wait_ge(o_act, strips)
            pe.wait_ge(o_dve, strips)
            merge_parts(strips)

        @block.scalar
        def _(act):
            def relu(s, b, g, k):
                n = s * groups + b * SLOTS + g
                step = 2 * (GROUP * n + k)
                for c in range(2):
                    act.wait_ge(rank_done, step + c + 1)
                    nc.scalar.activation(code[:, g, k, c * CHUNK:(c + 1) * CHUNK], rank_ps[c][:], ACT.Relu
                                         ).then_inc(relu_done, 1)

            def relu_direct(s, b, g, k, direct, before):
                step = 2 * (GROUP * (s * groups + b * SLOTS + g) + k)
                nth = (b - (blocks - direct)) * BLOCK_TILES + (g * GROUP + k)
                act.wait_ge(part_used, (s + 1) * 2 + before * BLOCK_TILES + nth - 1)
                for c in range(2):
                    act.wait_ge(rank_done, step + c + 1)
                    nc.scalar.activation(w_direct[:, k % 2, c * CHUNK:(c + 1) * CHUNK].bitcast(I16), rank_ps[c][:],
                                         ACT.Relu, scale=CODE_UNIT).then_inc(relu_done, 1)

            def store_codes(s, b, g):
                n = s * groups + b * SLOTS + g
                act.wait_ge(relu_done, 2 * GROUP * (n + 1))
                act.dma_start(codes[n], code[:, g].rearrange("p k i -> p (k i)")).then_inc(code_out[g], 16)

            def partial_copy(s, before):
                act.wait_ge(part_used, s * 2 + before * BLOCK_TILES)
                nc.scalar.activation(partial_t[:], part_ps[:], ACT.Copy).then_inc(part_ready, 1)

            def move_h(s, b, g, first, start):
                n = s * groups + b * SLOTS + g
                if first and not start:
                    act.wait_ge(h_ready, 4)
                if not (first and start and g < SLOTS):
                    act.wait_ge(l0_done, n - SLOTS + 1)
                wrapped = (tiles - GROUP * g) - b * BLOCK_TILES
                nc.scalar.activation(h_slot[:, g % SLOTS], h_wrap[:, bass.ds(wrapped, GROUP), :], ACT.Copy
                                     ).then_inc(h_moved, 1)

            def neigh_copy(s):
                act.wait_ge(l0_done, s * groups)
                nc.scalar.activation(neigh_t[:], l0_ps[:], ACT.Copy).then_inc(neigh_ready, 1)

            def ht_copy(s):
                act.wait_ge(ht_ps, s)
                nc.scalar.activation(feat_t[:], tr_ps[:], ACT.Relu).then_inc(ht_ready, 1)

            def h1t_copy(s):
                act.wait_ge(h1t_ps, s)
                nc.scalar.activation(feat_t[:], tr_ps[:], ACT.Relu).then_inc(h1t_ready, 1)

            def parts_of(s, part):
                return support[:, bass.ds((s - 1) * TILES, TILES), part * F:(part + 1) * F]

            def std(norm, count):
                act.wait_ge(var_ready, norm)
                nc.scalar.activation(st[:, 4, 0:count], st[:, 3, 0:count], ACT.Sqrt).then_inc(std_ready, 1)

            def x1_std(s):
                std(s + 4, TILES)

            def support_hi(s):
                act.wait_ge(sup_done, s)
                nc.scalar.activation(parts_of(s, 0), sup_ps[:].rearrange("p (t f) -> p t f", f=F), ACT.Copy
                                     ).then_inc(hi_done, 1)

            def support_lo(s):
                act.wait_ge(res_ready, s)
                nc.scalar.activation(parts_of(s, 1), t_b[:], ACT.Copy, scale=LO_SCALE).then_inc(lo_done, 1)

            end_at = {(0, 1): ht_copy, (1, 2): x1_std, (2, 2): h1t_copy, (3, 0): support_hi, (3, 2): support_lo}

            def sweep_block(s, b, first, start, before, stored_before):
                if start and not first:
                    neigh_copy(s)
                for g in range(SLOTS):
                    if not (first and start):
                        act.wait_ge(code_out[g], (stored_before + b) * 16)
                    for k in range(GROUP):
                        relu(s, b, g, k)
                        if k == 2:
                            move_h(s, b, g + 1, first, start)
                        if first and start and (g, k) in x_std_at:
                            std(x_std_at[g, k], chunk_tiles)
                        if start and not first:
                            if (g, k) == (1, 1):
                                partial_copy(s, before)
                            if (g, k) in end_at:
                                end_at[g, k](s)
                    store_codes(s, b, g)

            def direct_block(s, b, direct, before):
                for g in range(SLOTS):
                    for k in range(GROUP):
                        relu_direct(s, b, g, k, direct, before)
                        if k == 2:
                            move_h(s, b, g + 1, False, False)

            x_std_at = {(1, 1): 2, (2, 3): 3, (3, 3): 4}
            std(1, chunk_tiles)
            act.wait_ge(h_ready, 1)
            move_h(0, 0, 0, True, True)
            for s0, s1, direct, stored0, direct0 in runs:

                def strip(s):
                    first = s0 == 0
                    before = (s - s0) * direct + direct0
                    stored_before = (s - s0) * (blocks - direct) + stored0
                    sweep_block(s, 0, first, True, before, stored_before)
                    loop(act, 1, blocks - direct, lambda b: sweep_block(s, b, first, False, before, stored_before))
                    loop(act, blocks - direct, blocks, lambda b: direct_block(s, b, direct, before))

                loop(act, s0, s1, strip)
            neigh_copy(strips)
            partial_copy(strips, direct_total)

            end_late = {4: x1_std, 9: h1t_copy, 11: support_hi, 13: support_lo}

            def sums_out(s, done):
                act.wait_ge(l1_done, done)
                nc.scalar.activation(feat_o[0][:], rank_ps[0][:], ACT.Copy).then_inc(o_act, 1)

            def decode(b, g, before):
                m = (before + b) * SLOTS + g
                act.wait_ge(code_in[g], (before + b + 1) * 16)
                act.wait_ge(l1_done, m - SLOTS + 1)
                cols = slice(DVE_SHARE, GROUP * STRIP)
                nc.scalar.activation(adj[:, g, 2 * STRIP:4 * STRIP].bitcast(I16)[:, cols],
                                     adj[:, g, 0:STRIP].bitcast(U8)[:, cols], ACT.Copy, scale=CODE_UNIT
                                     ).then_inc(dec_act, 1)

            ht_copy(strips)
            for m in range(SLOTS, groups):
                decode(m // SLOTS, m % SLOTS, 0)
                if m in end_late:
                    end_late[m](strips)
            for s0, s1, direct, stored0, _ in runs[1:]:
                stored = blocks - direct

                def decode_strip(s):
                    before = (s - s0) * stored + stored0
                    for g in range(SLOTS):
                        decode(0, g, before)
                        if g == 2:
                            sums_out(s, before * SLOTS)
                    loop(act, 1, stored, lambda b: [decode(b, g, before) for g in range(SLOTS)])

                loop(act, s0, s1, decode_strip)
            sums_out(strips, stored_total * SLOTS)
            for q in range(SLOTS):
                act.wait_ge(code_out[q], 16 * stored_total)

        @block.vector
        def _(dve):
            def per_tile(col, count=TILES):
                return st[:, col, 0:count].unsqueeze(2).to_broadcast([P, count, F])

            LN_STEPS = 9

            def statistics(src, centred, squares, count, done):
                nc.vector.tensor_reduce(st[:, 0, 0:count], src, AX_X, ALU.add).then_inc(dve_step, 1)
                dve.wait_ge(dve_step, done + 1)
                nc.vector.tensor_scalar(st[:, 1, 0:count], st[:, 0, 0:count], 1.0 / F, None, ALU.mult).then_inc(dve_step, 1)
                dve.wait_ge(dve_step, done + 2)
                nc.vector.tensor_tensor(centred, src, per_tile(1, count), ALU.subtract).then_inc(dve_step, 1)
                dve.wait_ge(dve_step, done + 3)
                nc.vector.tensor_tensor(squares, centred, centred, ALU.mult).then_inc(dve_step, 1)
                dve.wait_ge(dve_step, done + 4)
                nc.vector.tensor_reduce(st[:, 2, 0:count], squares, AX_X, ALU.add).then_inc(dve_step, 1)
                dve.wait_ge(dve_step, done + 5)
                nc.vector.tensor_scalar(st[:, 3, 0:count], st[:, 2, 0:count], 1.0 / F, EPS, ALU.mult, ALU.add
                                        ).then_inc(var_ready, 1)

            def root(count, done, norm):
                dve.wait_ge(std_ready, norm)
                nc.vector.reciprocal(st[:, 5, 0:count], st[:, 4, 0:count]).then_inc(dve_step, 1)
                dve.wait_ge(dve_step, done + 6)
                nc.vector.scalar_tensor_tensor(st[:, 6, 0:count], st[:, 3, 0:count], -0.5, st[:, 5, 0:count],
                                               ALU.mult, ALU.mult).then_inc(dve_step, 1)
                dve.wait_ge(dve_step, done + 7)
                nc.vector.tensor_tensor(st[:, 7, 0:count], st[:, 6, 0:count], st[:, 5, 0:count], ALU.mult
                                        ).then_inc(dve_step, 1)
                dve.wait_ge(dve_step, done + 8)
                nc.vector.scalar_tensor_tensor(st[:, 8, 0:count], st[:, 7, 0:count], 1.5, st[:, 5, 0:count],
                                               ALU.add, ALU.mult).then_inc(dve_step, 1)
                dve.wait_ge(dve_step, done + 9)

            quarter = chunk_tiles * F

            def h_quarter(c):
                done = (3 - c) * LN_STEPS + (1 if c < 3 else 0)
                part = slice(c * chunk_tiles, (c + 1) * chunk_tiles)
                room = support[:].rearrange("p t f -> p (t f)").bitcast(F32)
                tmp = [room[:, q * quarter:(q + 1) * quarter].rearrange("p (t f) -> p t f", f=F) for q in range(3)]
                dve.wait_ge(x_in[c], 16)
                statistics(x_all[:, part, :], tmp[0], tmp[1], chunk_tiles, done)
                root(chunk_tiles, done, 4 - c)
                nc.vector.scalar_tensor_tensor(h_all[:, part, :], tmp[0], 0.0, per_tile(8, chunk_tiles), ALU.max, ALU.mult
                                               ).then_inc(h_ready, 1)
                if c == 3:
                    dve.wait_ge(h_ready, 1)
                    nc.vector.tensor_copy(h_wrap[:, 0:GROUP, :], h_all[:, tiles - GROUP:, :]).then_inc(dve_step, 1)

            def scale_weight(done):
                dve.wait_ge(par_in, 16 * 7)
                both = wn[:].rearrange("p a f -> p (a f)")
                nc.vector.tensor_reduce(wm[:, 0:1], both, AX_X, ALU.max).then_inc(dve_step, 1)
                nc.vector.tensor_reduce(wm[:, 1:2], both, AX_X, ALU.min).then_inc(dve_step, 1)
                dve.wait_ge(dve_step, done + 2)
                nc.vector.scalar_tensor_tensor(wm[:, 2:3], wm[:, 1:2], -1.0, wm[:, 0:1], ALU.mult, ALU.max
                                               ).then_inc(wmax_part, 1)
                dve.wait_ge(wmax_all, 1)
                nc.vector.tensor_scalar(wm[:, 4:5], wm[:, 3:4], 1e-30, None, ALU.max).then_inc(dve_step, 1)
                dve.wait_ge(dve_step, done + 3)
                nc.vector.reciprocal(wm[:, 5:6], wm[:, 4:5]).then_inc(dve_step, 1)
                dve.wait_ge(dve_step, done + 4)
                nc.vector.tensor_scalar(both, both, wm[:, 5:6], SUPPORT_SCALE, ALU.mult, ALU.mult).then_inc(dve_step, 1)
                nc.vector.tensor_scalar(merge[:], merge[:], wm[:, 4:5], None, ALU.mult).then_inc(dve_step, 1)

            setup_done = 4 * LN_STEPS + 1 + 6

            END_STEPS = 6 + LN_STEPS + 1

            def masks(s, b, g, first, start):
                n = s * groups + b * SLOTS + g
                dve.wait_ge(adj_in[g], 16 * (s * blocks + b + 1))
                if not (first and start and g < 2):
                    dve.wait_ge(rank_done, 2 * GROUP * (n - 1) + 2)
                nc.vector.tensor_scalar(mask[:, g % 2].rearrange("p k i -> p (k i)"), adj[:, g, :], 0.0, None,
                                        ALU.not_equal).then_inc(mask_ready, 1)

            def row_sums(s, b, g, first, start):
                n = s * groups + b * SLOTS + g
                if start and g == 0:
                    if not first:
                        dve.wait_ge(deg_ready, s)
                    nc.vector.tensor_copy(deg_acc[:], adj[:, g, :]).then_inc(deg_added, 1)
                else:
                    dve.wait_ge(deg_added, n)
                    nc.vector.tensor_tensor(deg_acc[:], deg_acc[:], adj[:, g, :], ALU.add).then_inc(deg_added, 1)

            def base(s):
                return setup_done + (s - 1) * END_STEPS

            def fold(s):
                dve.wait_ge(deg_added, s * groups)
                half = GROUP * STRIP // 2
                nc.vector.tensor_tensor(deg_acc[:, 0:half], deg_acc[:, 0:half], deg_acc[:, half:], ALU.add
                                        ).then_inc(dve_step, 1)
                dve.wait_ge(dve_step, base(s) + 1)
                nc.vector.tensor_tensor(deg_part[:], deg_acc[:, 0:STRIP], deg_acc[:, STRIP:half], ALU.add
                                        ).then_inc(deg_ready, 1)

            def x1_part(s):
                own = x_all[:, bass.ds((s - 1) * TILES, TILES), :]
                at = base(s)
                dve.wait_ge(lin_done, s)
                nc.vector.tensor_scalar(st[:, 9, 0:TILES], deg_ps[:, 0:TILES], 1.0, None, ALU.add).then_inc(dve_step, 1)
                dve.wait_ge(dve_step, at + 2)
                nc.vector.reciprocal(st[:, 10, 0:TILES], st[:, 9, 0:TILES]).then_inc(dve_step, 1)
                dve.wait_ge(dve_step, at + 3)
                nc.vector.tensor_tensor(t_a[:], agg_ps[:].rearrange("p (t f) -> p t f", f=F), per_tile(10), ALU.mult
                                        ).then_inc(dve_step, 1)
                dve.wait_ge(dve_step, at + 4)
                nc.vector.tensor_tensor(t_b[:], t_a[:], lin_ps.rearrange("p (t f) -> p t f", f=F), ALU.add
                                        ).then_inc(dve_step, 1)
                dve.wait_ge(dve_step, at + 5)
                nc.vector.tensor_tensor(t_a[:], t_b[:], own, ALU.add).then_inc(dve_step, 1)
                dve.wait_ge(dve_step, at + 6)
                statistics(t_a[:], t_b[:], t_c[:], TILES, at + 6)

            def h1_part(s):
                own = x_all[:, bass.ds((s - 1) * TILES, TILES), :]
                root(TILES, base(s) + 6, s + 4)
                nc.vector.tensor_tensor(t_c[:], t_b[:], per_tile(8), ALU.mult).then_inc(h1_ready, 1)
                nc.vector.tensor_tensor(own, t_a[:], bias_bc[:].unsqueeze(1).to_broadcast([P, TILES, F]), ALU.add
                                        ).then_inc(dve_step, 1)

            def residue(s):
                dve.wait_ge(hi_done, s)
                nc.vector.tensor_tensor(t_b[:], sup_ps[:].rearrange("p (t f) -> p t f", f=F),
                                        support[:, bass.ds((s - 1) * TILES, TILES), 0:F], ALU.subtract
                                        ).then_inc(res_ready, 1)
                dve.wait_ge(part_done, s)
                dve.wait_ge(dve_step, base(s) + END_STEPS)
                own = x_all[:, bass.ds((s - 1) * TILES, TILES), :]
                nc.vector.tensor_tensor(own, own, tr_ps[:].rearrange("p (t f) -> p t f", f=F), ALU.add
                                        ).then_inc(own_done, 1)

            def sweep_block(s, b, first, start):
                end = start and not first
                for g in range(SLOTS):
                    if end and g == 2:
                        x1_part(s)
                    masks(s, b, g, first, start)
                    if end and g == 0:
                        fold(s)
                    if end and g == 2:
                        h1_part(s)
                    row_sums(s, b, g, first, start)
                    if end and g == 3:
                        residue(s)

            h_quarter(3)
            masks(0, 0, 0, True, True)
            masks(0, 0, 1, True, True)
            row_sums(0, 0, 0, True, True)
            h_quarter(2)
            masks(0, 0, 2, True, True)
            row_sums(0, 0, 1, True, True)
            h_quarter(1)
            masks(0, 0, 3, True, True)
            row_sums(0, 0, 2, True, True)
            h_quarter(0)
            row_sums(0, 0, 3, True, True)
            loop(dve, 1, blocks, lambda b: sweep_block(0, b, True, False))
            scale_weight(4 * LN_STEPS + 1)
            with dve.Fori(1, strips) as s:
                sweep_block(s, 0, False, True)
                loop(dve, 1, blocks, lambda b: sweep_block(s, b, False, False))
            fold(strips)

            end_late = {3: lambda s: (x1_part(s), h1_part(s)), 12: residue}

            def sums_out(s, done):
                dve.wait_ge(l1_done, done)
                nc.vector.tensor_copy(feat_o[1], rank_ps[1][:]).then_inc(o_dve, 1)

            def result(s):
                dve.wait_ge(fin_ps, s)
                if not isinstance(s, int) or s > 1:
                    dve.wait_ge(out_done, (s - 1) * 16)
                nc.vector.tensor_tensor(t_a[:], agg_ps[:].rearrange("p (t f) -> p t f", f=F),
                                        x_all[:, bass.ds((s - 1) * TILES, TILES), :], ALU.add).then_inc(y_ready, 1)

            def decode(b, g, before, empty):
                m = (before + b) * SLOTS + g
                dve.wait_ge(code_in[g], (before + b + 1) * 16)
                if not empty:
                    dve.wait_ge(l1_done, m - SLOTS + 1)
                cols = slice(0, GROUP * STRIP if empty else DVE_SHARE)
                nc.vector.tensor_scalar(adj[:, g, 2 * STRIP:4 * STRIP].bitcast(I16)[:, cols],
                                        adj[:, g, 0:STRIP].bitcast(U8)[:, cols], CODE_UNIT, None, ALU.mult
                                        ).then_inc(dec_dve, 1)

            for m in range(groups):
                decode(m // SLOTS, m % SLOTS, 0, m < SLOTS)
                if m in end_late:
                    end_late[m](strips)
            dve.wait_ge(own_done, strips)
            for s0, s1, direct, stored0, _ in runs[1:]:
                stored = blocks - direct

                def decode_strip(s):
                    before = (s - s0) * stored + stored0
                    for g in range(SLOTS):
                        decode(0, g, before, False)
                        if g == 2:
                            sums_out(s, before * SLOTS)
                    result(s)
                    loop(dve, 1, stored, lambda b: [decode(b, g, before, False) for g in range(SLOTS)])

                loop(dve, s0, s1, decode_strip)
            sums_out(strips, stored_total * SLOTS)
            result(strips)


def kernel(x, adj, L0_gnn_W, L1_gnn_weight, L1_gnn_bias):
    import numpy as np
    import concourse.bacc as bacc
    from concourse.bass_utils import run_bass_kernel_spmd

    x, adj = np.asarray(x), np.asarray(adj)
    n = x.shape[0]
    strips, tiles = n // STRIP, n // P
    adj_t = adj.reshape(strips, STRIP, tiles // GROUP, GROUP, P)[:, :, ::-1, ::-1, :]
    arrays = {
        "x_t": np.ascontiguousarray(x.reshape(tiles, P, F).transpose(1, 0, 2)),
        "adj_t": np.ascontiguousarray(adj_t.transpose(0, 2, 4, 3, 1)).reshape(strips, tiles // GROUP, P, GROUP * STRIP),
        "w_t": np.ascontiguousarray(np.asarray(L0_gnn_W).T),
        "weight": np.ascontiguousarray(L1_gnn_weight),
        "bias": np.ascontiguousarray(L1_gnn_bias),
    }
    nc = bacc.Bacc("TRN2", target_bir_lowering=False, num_devices=1)
    args = [nc.dram_tensor(k, a.shape, mybir.dt.from_np(a.dtype), kind="ExternalInput").ap() for k, a in arrays.items()]
    args.append(nc.dram_tensor("out_t", (P, tiles, F), F32, kind="ExternalOutput").ap())
    build_program(nc, *args)
    result = run_bass_kernel_spmd(nc, [arrays], core_ids=[0])
    return np.ascontiguousarray(result.results[0]["out_t"].transpose(1, 0, 2)).reshape(n, F)
```

```python
from contextlib import ExitStack

import concourse.bass as bass
from concourse import mybir

ALU = mybir.AluOpType
ACT = mybir.ActivationFunctionType
AX_X = mybir.AxisListType.X
RMAX = bass.bass_isa.ReduceOp.max
F32 = mybir.dt.float32
BF16 = mybir.dt.bfloat16
F16 = mybir.dt.float16
U8 = mybir.dt.uint8
I16 = mybir.dt.int16

P = 128
F = 64
CHUNK = 512
STRIP = 2 * CHUNK
TILES = STRIP // P
GROUP = 4
SLOTS = 4
SUMS_AT = 2
MERGE_AT = 3
MAX_NEIGH = 100
EPS = 1e-5
SUPPORT_SCALE = 512.0
LO_SCALE = 2048.0
CODE_UNIT = 128.0
UNSCALE = 2.0 ** (127 - MAX_NEIGH) / SUPPORT_SCALE
PE_SUMS = 2
SQUARES_FROM = 2
DVE_SHARE = 2560


def build_program(nc, x_t, adj_t, w_t, weight, bias, out_t):
    strips, groups = adj_t.shape[0], adj_t.shape[1]
    tiles = groups * GROUP
    blocks = groups // SLOTS
    assert groups % SLOTS == 0 and blocks >= 2 and strips >= 2 and tiles == strips * TILES
    ends = [tiles * e // 64 for e in (64, 56, 48, 32, 16, 0)]
    pieces = [(ends[q + 1], ends[q]) for q in range(5)]

    def direct_blocks(s):
        return min(blocks - 1, s * TILES // (GROUP * SLOTS))

    runs = []
    for s in range(strips):
        if s > 1 and direct_blocks(s) == runs[-1][2]:
            runs[-1][1] = s + 1
        else:
            runs.append([s, s + 1, direct_blocks(s), sum(blocks - direct_blocks(q) for q in range(s)),
                         sum(direct_blocks(q) for q in range(s))])
    stored_in = [blocks - direct_blocks(s) for s in range(strips)]
    stored_before = [sum(stored_in[:s]) for s in range(strips)]
    stored_total = sum(blocks - direct_blocks(s) for s in range(strips))
    direct_total = sum(direct_blocks(s) for s in range(strips))
    BLOCK_TILES = GROUP * SLOTS

    def loop(engine, first, end, body):
        if end - first == 1:
            body(first)
        elif end > first:
            with engine.Fori(first, end) as i:
                body(i)

    codes = nc.dram_tensor("codes", (strips * groups, P, GROUP * STRIP), U8, kind="Internal").ap()
    adj_groups = adj_t.rearrange("s g p c -> (s g) p c")

    with ExitStack() as ctx:
        def sb(name, shape, dt):
            return ctx.enter_context(nc.sbuf_tensor(name, shape, dt))

        def psum(name):
            return ctx.enter_context(nc.psum_tensor(name, [P, CHUNK], F32))

        def sem(name):
            return ctx.enter_context(nc.semaphore(name))

        adj = sb("adj", [P, SLOTS, GROUP * STRIP], F32)
        mask = sb("mask", [P, 2, GROUP, STRIP], BF16)
        code = sb("code", [P, SLOTS, GROUP, STRIP], U8)
        deg_acc = sb("deg_acc", [P, GROUP * STRIP], F32)
        deg_part = sb("deg_part", [P, STRIP], F32)
        x_all = sb("x_all", [P, tiles, F], F32)
        h_wrap = sb("h_wrap", [P, GROUP + tiles, F], F32)
        h_all = h_wrap[:, GROUP:, :]
        h_slot = sb("h_slot", [P, SLOTS, GROUP, F], F32)
        h_strip = sb("h_strip", [P, TILES, F], F32)
        support = sb("support", [P, tiles, 2 * F], F16)
        neigh_t = sb("neigh_t", [P, CHUNK], F32)
        feat_t = sb("feat_t", [P, CHUNK], F32)
        w_direct = sb("w_direct", [P, 2, STRIP], BF16)
        partial_t = sb("partial_t", [P, STRIP], F32)
        t_a = sb("t_a", [P, TILES, F], F32)
        t_b = sb("t_b", [P, TILES, F], F32)
        t_c = sb("t_c", [P, TILES, F], F32)
        st = sb("st", [P, 11, 16], F32)
        ident = sb("ident", [P, P], F32)
        ones = sb("ones", [P, F], F32)
        half_ones = sb("half_ones", [P, 2], F32)
        here = sb("here", [P, P], BF16)
        carry = sb("carry", [P, P], BF16)
        zeros = sb("zeros", [P, CHUNK], BF16)
        w1 = sb("w1", [P, 2, F], F32)
        w2 = sb("w2", [P, 2, F], F32)
        wn = sb("wn", [P, 2, F], F32)
        merge = sb("merge", [P, F], F32)
        bias_bc = sb("bias_bc", [P, F], F32)
        wm = sb("wm", [P, 8], F32)

        pe_sums = w_direct[:].rearrange("p a c -> p (a c)").bitcast(F32)[:, 0:CHUNK]

        rank_ps = [psum("rank_a"), psum("rank_b")]
        l0_ps = psum("l0")
        tr_ps = psum("tr")
        agg_ps = psum("agg")
        sup_ps = psum("sup")
        part_ps = ctx.enter_context(nc.psum_tensor("part", [P, STRIP], F32))
        lin_ps = tr_ps[:]
        deg_ps = sup_ps[:, 0:TILES]

        x_in = [sem(f"x_in{q}") for q in range(len(pieces))]
        par_in = sem("par_in")
        adj_in = [sem(f"adj_in{g}") for g in range(SLOTS)]
        hs_in = sem("hs_in")
        code_out = [sem(f"code_out{g}") for g in range(SLOTS)]
        code_in = [sem(f"code_in{g}") for g in range(SLOTS)]
        out_done = [sem(f"out_done{half}") for half in range(2)]
        last_done = sem("last_done")
        sp_waits = sem("sp_waits")
        pool_chain = sem("pool_chain")
        consts = sem("consts")
        wmax_part = sem("wmax_part")
        wmax_all = sem("wmax_all")
        h_ready = sem("h_ready")
        squares_ready = sem("squares_ready")
        pe_sums_done = sem("pe_sums_done")
        pe_sums_ready = sem("pe_sums_ready")
        mask_ready = sem("mask_ready")
        deg_added = sem("deg_added")
        h_moved = sem("h_moved")
        rank_done = sem("rank_done")
        part_used = sem("part_used")
        relu_done = sem("relu_done")
        l0_done = sem("l0_done")
        neigh_ready = sem("neigh_ready")
        deg_ready = sem("deg_ready")
        ht_ps = sem("ht_ps")
        agg_done = sem("agg_done")
        ht_ready = sem("ht_ready")
        lin_done = sem("lin_done")
        h1_ready = sem("h1_ready")
        h1t_ps = sem("h1t_ps")
        h1t_ready = sem("h1t_ready")
        sup_done = sem("sup_done")
        hi_done = sem("hi_done")
        res_ready = sem("res_ready")
        lo_done = sem("lo_done")
        part_ready = sem("part_ready")
        part_done = sem("part_done")
        var_ready = sem("var_ready")
        std_ready = sem("std_ready")
        own_done = sem("own_done")
        dve_step = sem("dve_step")
        dec_dve = sem("dec_dve")
        dec_act = sem("dec_act")
        l1_done = sem("l1_done")
        o_act = sem("o_act")
        o_dve = sem("o_dve")
        fin_ps = sem("fin_ps")
        y_ready = sem("y_ready")

        feat_o = [neigh_t, deg_part[:, 0:CHUNK]]

        def mask_at(g, k):
            return mask[:, g % 2, k, :]

        LN_STEPS = 9

        def temporaries(count):
            room = support[:].rearrange("p t f -> p (t f)").bitcast(F32)
            return [room[:, q * count * F:(q + 1) * count * F].rearrange("p (t f) -> p t f", f=F) for q in range(2)]

        block = ctx.enter_context(nc.Block())

        @block.sync
        def _(sp):
            def wait(semaphore, count):
                sp.wait_ge(semaphore, count)
                sp.sem_inc(sp_waits, 1)

            for q, (t0, t1) in enumerate(pieces):
                sp.dma_start(x_all[:, t0:t1, :], x_t[:, t0:t1, :]).then_inc(x_in[q], 16)
                if 1 <= q <= SLOTS:
                    sp.dma_start(adj[:, q - 1, :], adj_groups[q - 1]).then_inc(adj_in[q - 1], 16)
            sp.wait_ge(consts, 1)
            for half in range(2):
                rows = slice(half * F, half * F + F)
                sp.dma_start(w1[rows, half, :], w_t[0:F, :]).then_inc(par_in, 16)
                sp.dma_start(w2[rows, half, :], w_t[F:2 * F, :]).then_inc(par_in, 16)
                sp.dma_start(wn[rows, half, :], weight).then_inc(par_in, 16)
            sp.dma_start(bias_bc[:], bias.partition_broadcast(P)).then_inc(par_in, 16)

            def load_block(s, b):
                for g in range(SLOTS):
                    n = s * groups + b * SLOTS + g
                    wait(mask_ready, n - SLOTS + 1)
                    if not isinstance(n, int) or n >= SLOTS + PE_SUMS:
                        wait(deg_added, n - SLOTS + 1 - PE_SUMS)
                    wait(l0_done, n - SLOTS + 1)
                    sp.dma_start(adj[:, g, :], adj_groups[n]).then_inc(adj_in[g], 16)

            load_block(0, 1)
            sp.wait_ge(h_ready, len(pieces))
            sp.dma_start(h_strip[:], h_all[:, 0:TILES, :]).then_inc(hs_in, 16)
            loop(sp, 2, blocks, lambda b: load_block(0, b))
            with sp.Fori(1, strips) as s:
                load_block(s, 0)
                wait(ht_ps, s)
                sp.dma_start(h_strip[:], h_all[:, bass.ds(s * TILES, TILES), :]).then_inc(hs_in, 16)
                loop(sp, 1, blocks, lambda b: load_block(s, b))

            total = strips * groups

            def load_codes(s, b, stored, before, prefetch):
                for g in range(SLOTS):
                    m = (before + b) * SLOTS + g
                    if prefetch:
                        last = total - SLOTS + g + 1
                        sp.wait_ge(mask_ready, last)
                        sp.wait_ge(deg_added, last - PE_SUMS)
                        sp.wait_ge(l0_done, last)
                    else:
                        wait(dec_dve, m - SLOTS + 1)
                        if not isinstance(m, int) or m >= 2 * SLOTS:
                            wait(dec_act, m + 1 - 2 * SLOTS)
                    sp.dma_start(adj[:, g, 0:STRIP].bitcast(U8), codes[s * groups + (stored * SLOTS - 1 - g) - b * SLOTS]
                                 ).then_inc(code_in[g], 16)

            for q in range(SLOTS):
                sp.wait_ge(code_out[q], 16 * blocks)
            load_codes(0, 0, blocks, 0, True)
            load_codes(0, 1, blocks, 0, False)
            loop(sp, 2, blocks, lambda b: load_codes(0, b, blocks, 0, False))
            for q in range(SLOTS):
                sp.wait_ge(code_out[q], 16 * stored_total)
            for s0, s1, direct, stored0, _ in runs[1:]:
                stored = blocks - direct

                def codes_of(s):
                    before = (s - s0) * stored + stored0
                    load_codes(s, 0, stored, before, False)
                    loop(sp, 1, stored, lambda b: load_codes(s, b, stored, before, False))

                loop(sp, s0, s1, codes_of)
            last = strips - 1
            sp.wait_ge(y_ready, strips)
            sp.dma_start(out_t[:, last * TILES:, :], t_a[:] if last % 2 == 0 else t_c[:]).then_inc(last_done, 16)
            sp.wait_ge(last_done, 16)

        @block.gpsimd
        def _(pool):
            steps = [0]

            def link(ins):
                steps[0] += 1
                ins.then_inc(pool_chain, 1)
                pool.wait_ge(pool_chain, steps[0])

            def diagonal(t, value, base):
                link(nc.gpsimd.affine_select(out=t, in_=t, compare_op=ALU.not_equal, fill=value, base=base,
                                             pattern=[[-1, t.shape[1]]], channel_multiplier=1))

            link(nc.gpsimd.memset(here[:], -1.0))
            link(nc.gpsimd.affine_select(out=here[:], in_=here[:], compare_op=ALU.is_gt, fill=0.0, base=0,
                                         pattern=[[-1, P]], channel_multiplier=1))
            diagonal(here[:], float(MAX_NEIGH), 0)
            link(nc.gpsimd.memset(carry[:], -1.0))
            link(nc.gpsimd.affine_select(out=carry[:], in_=carry[:], compare_op=ALU.is_gt, fill=0.0, base=0,
                                         pattern=[[1, P]], channel_multiplier=-1))
            diagonal(carry[:], -1.0 - MAX_NEIGH, 0)
            for matrix in (zeros, w1, w2, wn, ident, half_ones):
                link(nc.gpsimd.memset(matrix[:], 0.0))
            diagonal(ident[:], 1.0, 0)
            link(nc.gpsimd.memset(ones[:], 1.0))
            for half in range(2):
                link(nc.gpsimd.memset(half_ones[half * F:half * F + F, half:half + 1], 1.0))
            link(nc.gpsimd.memset(merge[:], 0.0))
            diagonal(merge[:], UNSCALE, 0)
            diagonal(merge[:], UNSCALE / LO_SCALE, -F)
            nc.gpsimd.nop().then_inc(consts, 1)
            pool.wait_ge(wmax_part, 1)
            nc.gpsimd.partition_all_reduce(wm[:, 3:4], wm[:, 2:3], P, RMAX).then_inc(wmax_all, 1)
            for s in range(strips - 1):
                pool.wait_ge(y_ready, s + 1)
                pool.dma_start(out_t[:, s * TILES:(s + 1) * TILES, :], t_a[:] if s % 2 == 0 else t_c[:]
                               ).then_inc(out_done[s % 2], 16)
            for half in range(2):
                pool.wait_ge(out_done[half], 16 * ((strips - half) // 2))

        @block.tensor
        def _(pe):
            def rank(s, b, g, k, first, start):
                n = s * groups + b * SLOTS + g
                step = 2 * (GROUP * n + k)
                if k == 0:
                    pe.wait_ge(mask_ready, n + 1)
                for c in range(2):
                    cols = slice(c * CHUNK, (c + 1) * CHUNK)
                    if not (first and start):
                        pe.wait_ge(relu_done, step + c - 1)
                    if not start:
                        prev = mask_at(g, k - 1) if k else mask_at(g + 1, GROUP - 1)
                        nc.tensor.matmul(rank_ps[c][:], carry[:], prev[:, cols], start=False, stop=True,
                                         skip_group_check=True)
                    nc.tensor.matmul(rank_ps[c][:], here[:], mask_at(g, k)[:, cols], start=start, stop=True,
                                     skip_group_check=True).then_inc(rank_done, 1)

            def l0(s, b, g, k, first, start, opening_sums):
                n = s * groups + b * SLOTS + g
                if k == 0:
                    pe.wait_ge(adj_in[g], 16 * (s * blocks + b + 1))
                    pe.wait_ge(h_moved, n + 1)
                if start and not first:
                    pe.wait_ge(neigh_ready, s)
                for c in range(2):
                    cols = slice(k * STRIP + c * CHUNK, k * STRIP + (c + 1) * CHUNK)
                    if opening_sums and g < PE_SUMS:
                        ins = nc.tensor.matmul(agg_ps[F * c:F * c + F, :], ones[:], adj[:, g, cols],
                                               start=g == 0 and k == 0, stop=True, skip_group_check=True)
                        if g == PE_SUMS - 1 and k == GROUP - 1 and c == 1:
                            ins.then_inc(pe_sums_done, 1)
                    ins = nc.tensor.matmul(l0_ps[F * c:F * c + F, :], h_slot[:, g, GROUP - 1 - k, :],
                                           adj[:, g, cols], start=start, stop=True, skip_group_check=True)
                if k == GROUP - 1:
                    ins.then_inc(l0_done, 1)

            def in_half(t):
                return slice((t % 4) * P, (t % 4 + 1) * P)

            def in_pair(t):
                return slice((t // 2) * P, (t // 2 + 1) * P)

            def transposes(nodes):
                for t in range(0, TILES, 2):
                    ins = nc.tensor.matmul(tr_ps[:, in_pair(t)], nodes[:, t:t + 2, :].rearrange("p t f -> p (t f)"), ident[:],
                                           start=True, stop=True)
                return ins

            def pair_products(out, matrix):
                for t in range(0, TILES, 2):
                    ins = nc.tensor.matmul(out[:, t * F:(t + 2) * F], feat_t[:, in_pair(t)],
                                           matrix[:].rearrange("p a f -> p (a f)"), start=True, stop=True)
                return ins

            def end_products(s):
                pe.wait_ge(hs_in, 16 * s)
                ins = transposes(h_strip)
                ins.then_inc(ht_ps, 1)
                pe.wait_ge(neigh_ready, s)
                for t in range(TILES // 2):
                    both = agg_ps[:].rearrange("p (half t f) -> p half t f", half=2, f=F)[:, :, t, :]
                    ins = nc.tensor.matmul(both, neigh_t[:, in_half(t)], w2[:], start=True, stop=True)
                ins.then_inc(agg_done, 1)

            def end_linear(s):
                pe.wait_ge(deg_ready, s)
                if not isinstance(s, int) or s > 1:
                    pe.wait_ge(res_ready, s - 1)
                if isinstance(s, int) and s == 1:
                    pe.wait_ge(pe_sums_ready, 1)
                for t in range(TILES):
                    nc.tensor.matmul(deg_ps[:, t:t + 1], deg_part[:, t * P:(t + 1) * P], ones[:, 0:1],
                                     start=True, stop=True, skip_group_check=True)
                    if isinstance(s, int) and s == 1:
                        nc.tensor.matmul(deg_ps[:, t:t + 1], pe_sums[:, in_half(t)], half_ones[:, t // 4:t // 4 + 1],
                                         start=False, stop=True, skip_group_check=True)
                pe.wait_ge(ht_ready, s)
                ins = pair_products(lin_ps, w1)
                ins.then_inc(lin_done, 1)

            def end_h1t(s):
                pe.wait_ge(h1_ready, s)
                ins = transposes(t_c)
                ins.then_inc(h1t_ps, 1)

            def end_support(s):
                pe.wait_ge(h1t_ready, s)
                ins = pair_products(sup_ps, wn)
                ins.then_inc(sup_done, 1)

            def end_partial(s):
                pe.wait_ge(part_ready, s)
                for t in range(TILES):
                    ins = nc.tensor.matmul(tr_ps[:, t * F:(t + 1) * F], partial_t[:, t * P:(t + 1) * P], merge[:],
                                           start=True, stop=True)
                ins.then_inc(part_done, 1)

            end_at = {(0, 0): [end_products], (0, 2): [end_linear], (2, 1): [end_h1t], (2, 3): [end_support, end_partial]}

            def clear_direct():
                for c in range(2):
                    nc.tensor.matmul(part_ps[:, c * CHUNK:(c + 1) * CHUNK], zeros[:, 0:P], zeros[:],
                                     start=True, stop=True, skip_group_check=True).then_inc(part_used, 1)

            def l1_direct(s, b, g, k, opening):
                step = 2 * (GROUP * (s * groups + b * SLOTS + g) + k)
                parts = support_of(b * -BLOCK_TILES + (tiles - 1 - g * GROUP - k))
                for c in range(2):
                    cols = slice(c * CHUNK, (c + 1) * CHUNK)
                    if opening and c == 0:
                        pe.wait_ge(part_ready, s)
                    pe.wait_ge(relu_done, step + c + 1)
                    ins = nc.tensor.matmul(part_ps[:, cols], parts, w_direct[:, k % 2, cols],
                                           start=opening, stop=True, skip_group_check=True)
                ins.then_inc(part_used, 1)

            def support_of(tile):
                return support[:, bass.ds(tile, 1), :].rearrange("p a f -> p (a f)")

            def sweep_block(s, b, first, start, direct=False, open_direct=False):
                for g in range(SLOTS):
                    for k in range(GROUP):
                        opening = start and g == 0 and k == 0
                        rank(s, b, g, k, first, opening)
                        l0(s, b, g, k, first, opening, first and start)
                        if direct:
                            l1_direct(s, b, g, k, open_direct and g == 0 and k == 0)
                        if start and not first:
                            for part in end_at.get((g, k), []):
                                part(s)

            pe.wait_ge(consts, 1)
            for s0, s1, direct, _, _ in runs:

                def strip(s):
                    first = s0 == 0
                    sweep_block(s, 0, first, True)
                    loop(pe, 1, blocks - direct, lambda b: sweep_block(s, b, first, False))
                    if direct:
                        pe.wait_ge(lo_done, s)
                        sweep_block(s, blocks - direct, False, False, True, True)
                        loop(pe, blocks - direct + 1, blocks, lambda b: sweep_block(s, b, False, False, True))
                    elif first:
                        clear_direct()

                loop(pe, s0, s1, strip)
                if s0 == 0:
                    pe.wait_ge(par_in, 16 * 7)

            o_ps = [[rank_ps[0][:], rank_ps[1][:]], [part_ps[:, 0:CHUNK], part_ps[:, CHUNK:STRIP]]]
            end_late = {0: [end_linear], 7: [end_h1t], 9: [end_support, end_partial]}

            def product_group(s, b, g, stored, before, start):
                m = b * SLOTS + (before * SLOTS + g)
                pe.wait_ge(dec_dve, m + 1)
                if not isinstance(m, int) or m >= SLOTS:
                    pe.wait_ge(dec_act, m + 1 - SLOTS)
                w = adj[:, g, 2 * STRIP:4 * STRIP].bitcast(BF16)
                for k in reversed(range(GROUP)):
                    tile = b * BLOCK_TILES + (tiles - stored * BLOCK_TILES + g * GROUP + (GROUP - 1 - k))
                    for c in range(2):
                        ins = nc.tensor.matmul(o_ps[s % 2][c], support_of(tile),
                                               w[:, k * STRIP + c * CHUNK:k * STRIP + (c + 1) * CHUNK],
                                               start=start and g == 0 and k == GROUP - 1, stop=True,
                                               skip_group_check=True)
                ins.then_inc(l1_done, 1)

            def product_block(s, b, stored, before, start):
                if start and s == 1:
                    pe.wait_ge(part_ready, strips)
                elif start:
                    pe.wait_ge(o_act, s - 1)
                    pe.wait_ge(o_dve, s - 1)
                for g in range(SLOTS):
                    product_group(s, b, g, stored, before, start)
                    if start and g == MERGE_AT:
                        merge_parts(s)

            def merge_parts(s):
                pe.wait_ge(o_act, s)
                pe.wait_ge(o_dve, s)
                for t in range(TILES):
                    ins = nc.tensor.matmul(agg_ps[:, t * F:(t + 1) * F], feat_o[t // 4][:, (t % 4) * P:(t % 4 + 1) * P],
                                           merge[:], start=True, stop=True)
                ins.then_inc(fin_ps, 1)

            pe.wait_ge(relu_done, 2 * tiles * strips)
            pe.wait_ge(lo_done, strips - 1)
            end_products(strips)
            for m in range(groups):
                if m == groups - TILES // GROUP:
                    pe.wait_ge(lo_done, strips)
                product_group(0, m // SLOTS, m % SLOTS, blocks, 0, m == 0)
                for part in end_late.get(m, []):
                    part(strips)
            for s in range(1, strips):
                product_block(s, 0, stored_in[s], stored_before[s], True)
                loop(pe, 1, stored_in[s], lambda b: product_block(s, b, stored_in[s], stored_before[s], False))
            merge_parts(strips)

        @block.scalar
        def _(act):
            def relu(s, b, g, k):
                n = s * groups + b * SLOTS + g
                step = 2 * (GROUP * n + k)
                for c in range(2):
                    act.wait_ge(rank_done, step + c + 1)
                    nc.scalar.activation(code[:, g, k, c * CHUNK:(c + 1) * CHUNK], rank_ps[c][:], ACT.Relu
                                         ).then_inc(relu_done, 1)

            def relu_direct(s, b, g, k, direct, before):
                step = 2 * (GROUP * (s * groups + b * SLOTS + g) + k)
                nth = (b - (blocks - direct)) * BLOCK_TILES + (g * GROUP + k)
                act.wait_ge(part_used, before * BLOCK_TILES + nth + 1)
                for c in range(2):
                    act.wait_ge(rank_done, step + c + 1)
                    nc.scalar.activation(w_direct[:, k % 2, c * CHUNK:(c + 1) * CHUNK].bitcast(I16), rank_ps[c][:],
                                         ACT.Relu, scale=CODE_UNIT).then_inc(relu_done, 1)

            def store_codes(s, b, g):
                n = s * groups + b * SLOTS + g
                act.wait_ge(relu_done, 2 * GROUP * (n + 1))
                act.dma_start(codes[n], code[:, g].rearrange("p k i -> p (k i)")).then_inc(code_out[g], 16)

            def partial_copy(s, before):
                act.wait_ge(part_used, 2 + before * BLOCK_TILES)
                nc.scalar.activation(partial_t[:], part_ps[:], ACT.Copy).then_inc(part_ready, 1)

            def move_h(s, b, g, first, start):
                n = s * groups + b * SLOTS + g
                if first:
                    tile = tiles - GROUP * (n + 1) if isinstance(n, int) and n < 3 * SLOTS else 0
                    act.wait_ge(h_ready, min(q + 1 for q in range(len(pieces)) if pieces[q][0] <= tile))
                if not (first and start and g < SLOTS):
                    act.wait_ge(l0_done, n - SLOTS + 1)
                wrapped = (tiles - GROUP * g) - b * BLOCK_TILES
                nc.scalar.activation(h_slot[:, g % SLOTS], h_wrap[:, bass.ds(wrapped, GROUP), :], ACT.Copy
                                     ).then_inc(h_moved, 1)

            def neigh_copy(s):
                act.wait_ge(l0_done, s * groups)
                nc.scalar.activation(neigh_t[:], l0_ps[:], ACT.Copy).then_inc(neigh_ready, 1)

            def ht_copy(s):
                act.wait_ge(ht_ps, s)
                nc.scalar.activation(feat_t[:], tr_ps[:], ACT.Relu).then_inc(ht_ready, 1)

            def h1t_copy(s):
                act.wait_ge(h1t_ps, s)
                nc.scalar.activation(feat_t[:], tr_ps[:], ACT.Relu).then_inc(h1t_ready, 1)

            def parts_of(s, part):
                return support[:, bass.ds((s - 1) * TILES, TILES), part * F:(part + 1) * F]

            def std(norm, count):
                act.wait_ge(var_ready, norm)
                nc.scalar.activation(st[:, 4, 0:count], st[:, 3, 0:count], ACT.Sqrt).then_inc(std_ready, 1)

            def x1_std(s):
                std(s + len(pieces), TILES)

            def support_hi(s):
                act.wait_ge(sup_done, s)
                nc.scalar.activation(parts_of(s, 0), sup_ps[:].rearrange("p (t f) -> p t f", f=F), ACT.Copy
                                     ).then_inc(hi_done, 1)

            def support_lo(s):
                act.wait_ge(res_ready, s)
                nc.scalar.activation(parts_of(s, 1), t_b[:], ACT.Copy, scale=LO_SCALE).then_inc(lo_done, 1)

            end_at = {(0, 1): ht_copy, (1, 2): x1_std, (2, 2): h1t_copy, (3, 0): support_hi, (3, 2): support_lo}

            def sweep_block(s, b, first, start, before, stored_before):
                if start and not first:
                    neigh_copy(s)
                for g in range(SLOTS):
                    if not (first and start):
                        act.wait_ge(code_out[g], (stored_before + b) * 16)
                    for k in range(GROUP):
                        relu(s, b, g, k)
                        if k == 2:
                            move_h(s, b, g + 1, first, start)
                        if first and isinstance(b, int) and (b * SLOTS + g, k) in squares_at:
                            piece_squares(squares_at[b * SLOTS + g, k])
                        if first and isinstance(b, int) and (b * SLOTS + g, k) in x_std_at:
                            piece_std(x_std_at[b * SLOTS + g, k])
                        if first and start and g * GROUP + k == PE_SUMS * GROUP:
                            act.wait_ge(pe_sums_done, 1)
                            nc.scalar.activation(pe_sums, agg_ps[:], ACT.Copy, scale=1.0 / F).then_inc(pe_sums_ready, 1)
                        if start and not first:
                            if (g, k) == (1, 1):
                                partial_copy(s, before)
                            if (g, k) in end_at:
                                end_at[g, k](s)
                    store_codes(s, b, g)

            def direct_block(s, b, direct, before):
                for g in range(SLOTS):
                    for k in range(GROUP):
                        relu_direct(s, b, g, k, direct, before)
                        if k == 2:
                            move_h(s, b, g + 1, False, False)

            def piece_squares(q):
                count = pieces[q][1] - pieces[q][0]
                centred, squares = temporaries(count)
                act.wait_ge(dve_step, q * LN_STEPS + 1 - (q - SQUARES_FROM) + 3)
                nc.scalar.activation(squares, centred, ACT.Square).then_inc(squares_ready, 1)

            def piece_std(q):
                std(q + 1, pieces[q][1] - pieces[q][0])

            x_std_at = {(0, 1): 1, (1, 2): 2, (3, 0): 3, (6, 1): 4}
            squares_at = {(1, 0): 2, (2, 2): 3, (5, 2): 4}
            piece_std(0)
            move_h(0, 0, 0, True, True)
            for s0, s1, direct, stored0, direct0 in runs:

                def strip(s):
                    first = s0 == 0
                    before = (s - s0) * direct + direct0
                    stored_before = (s - s0) * (blocks - direct) + stored0
                    sweep_block(s, 0, first, True, before, stored_before)
                    if first:
                        sweep_block(s, 1, True, False, before, stored_before)
                    loop(act, 2 if first else 1, blocks - direct,
                         lambda b: sweep_block(s, b, first, False, before, stored_before))
                    loop(act, blocks - direct, blocks, lambda b: direct_block(s, b, direct, before))

                loop(act, s0, s1, strip)
            neigh_copy(strips)
            partial_copy(strips, direct_total)

            end_late = {6: x1_std, 9: h1t_copy, 11: support_hi, 13: support_lo}

            def sums_out(s, done):
                act.wait_ge(l1_done, done)
                if s > 1:
                    act.wait_ge(fin_ps, s - 1)
                nc.scalar.activation(feat_o[0][:], rank_ps[0][:] if s % 2 else part_ps[:, 0:CHUNK], ACT.Copy
                                     ).then_inc(o_act, 1)

            def decode(b, g, before):
                m = (before + b) * SLOTS + g
                act.wait_ge(code_in[g], (before + b + 1) * 16)
                act.wait_ge(l1_done, m - SLOTS + 1)
                cols = slice(DVE_SHARE, GROUP * STRIP)
                nc.scalar.activation(adj[:, g, 2 * STRIP:4 * STRIP].bitcast(I16)[:, cols],
                                     adj[:, g, 0:STRIP].bitcast(U8)[:, cols], ACT.Copy, scale=CODE_UNIT
                                     ).then_inc(dec_act, 1)

            ht_copy(strips)
            for m in range(SLOTS, groups):
                decode(m // SLOTS, m % SLOTS, 0)
                if m in end_late:
                    end_late[m](strips)
            for s in range(1, strips):
                before = stored_before[s]
                for g in range(SLOTS):
                    decode(0, g, before)
                    if g == SUMS_AT:
                        sums_out(s, before * SLOTS)
                loop(act, 1, stored_in[s], lambda b: [decode(b, g, before) for g in range(SLOTS)])
            sums_out(strips, stored_total * SLOTS)
            for q in range(SLOTS):
                act.wait_ge(code_out[q], 16 * stored_total)

        @block.vector
        def _(dve):
            def per_tile(col, count=TILES):
                return st[:, col, 0:count].unsqueeze(2).to_broadcast([P, count, F])

            def centre(src, centred, count, done):
                nc.vector.tensor_reduce(st[:, 0, 0:count], src, AX_X, ALU.add).then_inc(dve_step, 1)
                dve.wait_ge(dve_step, done + 1)
                nc.vector.tensor_scalar(st[:, 1, 0:count], st[:, 0, 0:count], 1.0 / F, None, ALU.mult).then_inc(dve_step, 1)
                dve.wait_ge(dve_step, done + 2)
                nc.vector.tensor_tensor(centred, src, per_tile(1, count), ALU.subtract).then_inc(dve_step, 1)

            def variance(squares, count, done):
                nc.vector.tensor_reduce(st[:, 2, 0:count], squares, AX_X, ALU.add).then_inc(dve_step, 1)
                dve.wait_ge(dve_step, done + 5)
                nc.vector.tensor_scalar(st[:, 3, 0:count], st[:, 2, 0:count], 1.0 / F, EPS, ALU.mult, ALU.add
                                        ).then_inc(var_ready, 1)

            def statistics(src, centred, squares, count, done):
                centre(src, centred, count, done)
                dve.wait_ge(dve_step, done + 3)
                nc.vector.tensor_tensor(squares, centred, centred, ALU.mult).then_inc(dve_step, 1)
                dve.wait_ge(dve_step, done + 4)
                variance(squares, count, done)

            def root(count, done, norm):
                dve.wait_ge(std_ready, norm)
                nc.vector.reciprocal(st[:, 5, 0:count], st[:, 4, 0:count]).then_inc(dve_step, 1)
                dve.wait_ge(dve_step, done + 6)
                nc.vector.scalar_tensor_tensor(st[:, 6, 0:count], st[:, 3, 0:count], -0.5, st[:, 5, 0:count],
                                               ALU.mult, ALU.mult).then_inc(dve_step, 1)
                dve.wait_ge(dve_step, done + 7)
                nc.vector.tensor_tensor(st[:, 7, 0:count], st[:, 6, 0:count], st[:, 5, 0:count], ALU.mult
                                        ).then_inc(dve_step, 1)
                dve.wait_ge(dve_step, done + 8)
                nc.vector.scalar_tensor_tensor(st[:, 8, 0:count], st[:, 7, 0:count], 1.5, st[:, 5, 0:count],
                                               ALU.add, ALU.mult).then_inc(dve_step, 1)
                dve.wait_ge(dve_step, done + 9)

            def piece_of(q):
                t0, t1 = pieces[q]
                return slice(t0, t1), t1 - t0, temporaries(t1 - t0), q * LN_STEPS + (1 if q > 0 else 0) - max(q - SQUARES_FROM, 0)

            def piece_statistics(q):
                part, count, tmp, done = piece_of(q)
                dve.wait_ge(x_in[q], 16)
                if q < SQUARES_FROM:
                    statistics(x_all[:, part, :], tmp[0], tmp[1], count, done)
                else:
                    centre(x_all[:, part, :], tmp[0], count, done)

            def piece_variance(q):
                part, count, tmp, done = piece_of(q)
                dve.wait_ge(squares_ready, q - SQUARES_FROM + 1)
                variance(tmp[1], count, done - 1)

            def piece_h(q):
                part, count, tmp, done = piece_of(q)
                root(count, done - (1 if q >= SQUARES_FROM else 0), q + 1)
                nc.vector.scalar_tensor_tensor(h_all[:, part, :], tmp[0], 0.0, per_tile(8, count), ALU.max, ALU.mult
                                               ).then_inc(h_ready, 1)
                if q == 0:
                    dve.wait_ge(h_ready, 1)
                    nc.vector.tensor_copy(h_wrap[:, 0:GROUP, :], h_all[:, tiles - GROUP:, :]).then_inc(dve_step, 1)

            def scale_weight(done):
                dve.wait_ge(par_in, 16 * 7)
                both = wn[:].rearrange("p a f -> p (a f)")
                nc.vector.tensor_reduce(wm[:, 0:1], both, AX_X, ALU.max).then_inc(dve_step, 1)
                nc.vector.tensor_reduce(wm[:, 1:2], both, AX_X, ALU.min).then_inc(dve_step, 1)
                dve.wait_ge(dve_step, done + 2)
                nc.vector.scalar_tensor_tensor(wm[:, 2:3], wm[:, 1:2], -1.0, wm[:, 0:1], ALU.mult, ALU.max
                                               ).then_inc(wmax_part, 1)
                dve.wait_ge(wmax_all, 1)
                nc.vector.tensor_scalar(wm[:, 4:5], wm[:, 3:4], 1e-30, None, ALU.max).then_inc(dve_step, 1)
                dve.wait_ge(dve_step, done + 3)
                nc.vector.reciprocal(wm[:, 5:6], wm[:, 4:5]).then_inc(dve_step, 1)
                dve.wait_ge(dve_step, done + 4)
                nc.vector.tensor_scalar(both, both, wm[:, 5:6], SUPPORT_SCALE, ALU.mult, ALU.mult).then_inc(dve_step, 1)
                nc.vector.tensor_scalar(merge[:], merge[:], wm[:, 4:5], None, ALU.mult).then_inc(dve_step, 1)

            setup_done = len(pieces) * LN_STEPS + 1 - (len(pieces) - SQUARES_FROM) + 6

            END_STEPS = 6 + LN_STEPS + 1

            def masks(s, b, g, first, start):
                n = s * groups + b * SLOTS + g
                dve.wait_ge(adj_in[g], 16 * (s * blocks + b + 1))
                if not (first and start and g < 2):
                    dve.wait_ge(rank_done, 2 * GROUP * (n - 1) + 2)
                nc.vector.tensor_scalar(mask[:, g % 2].rearrange("p k i -> p (k i)"), adj[:, g, :], 0.0, None,
                                        ALU.not_equal).then_inc(mask_ready, 1)

            def row_sums(s, b, g, first, start):
                n = s * groups + b * SLOTS + g
                if start and g == (PE_SUMS if first else 0):
                    if not first:
                        dve.wait_ge(deg_ready, s)
                    nc.vector.tensor_copy(deg_acc[:], adj[:, g, :]).then_inc(deg_added, 1)
                else:
                    dve.wait_ge(deg_added, n - PE_SUMS)
                    nc.vector.tensor_tensor(deg_acc[:], deg_acc[:], adj[:, g, :], ALU.add).then_inc(deg_added, 1)

            def base(s):
                return setup_done + (s - 1) * END_STEPS

            def fold(s):
                dve.wait_ge(deg_added, s * groups - PE_SUMS)
                half = GROUP * STRIP // 2
                nc.vector.tensor_tensor(deg_acc[:, 0:half], deg_acc[:, 0:half], deg_acc[:, half:], ALU.add
                                        ).then_inc(dve_step, 1)
                dve.wait_ge(dve_step, base(s) + 1)
                nc.vector.tensor_tensor(deg_part[:], deg_acc[:, 0:STRIP], deg_acc[:, STRIP:half], ALU.add
                                        ).then_inc(deg_ready, 1)

            def x1_sum(s):
                own = x_all[:, bass.ds((s - 1) * TILES, TILES), :]
                at = base(s)
                dve.wait_ge(lin_done, s)
                nc.vector.tensor_scalar(st[:, 9, 0:TILES], deg_ps[:, 0:TILES], 1.0, None, ALU.add).then_inc(dve_step, 1)
                dve.wait_ge(dve_step, at + 2)
                nc.vector.reciprocal(st[:, 10, 0:TILES], st[:, 9, 0:TILES]).then_inc(dve_step, 1)
                dve.wait_ge(dve_step, at + 3)
                nc.vector.tensor_tensor(t_a[:], agg_ps[:].rearrange("p (t f) -> p t f", f=F), per_tile(10), ALU.mult
                                        ).then_inc(dve_step, 1)
                dve.wait_ge(dve_step, at + 4)
                nc.vector.tensor_tensor(t_b[:], t_a[:], lin_ps.rearrange("p (t f) -> p t f", f=F), ALU.add
                                        ).then_inc(dve_step, 1)
                dve.wait_ge(dve_step, at + 5)
                nc.vector.tensor_tensor(t_a[:], t_b[:], own, ALU.add).then_inc(dve_step, 1)

            def x1_statistics(s):
                dve.wait_ge(dve_step, base(s) + 6)
                statistics(t_a[:], t_b[:], t_c[:], TILES, base(s) + 6)

            def h1_part(s):
                own = x_all[:, bass.ds((s - 1) * TILES, TILES), :]
                root(TILES, base(s) + 6, s + len(pieces))
                nc.vector.tensor_tensor(t_c[:], t_b[:], per_tile(8), ALU.mult).then_inc(h1_ready, 1)
                nc.vector.tensor_tensor(own, t_a[:], bias_bc[:].unsqueeze(1).to_broadcast([P, TILES, F]), ALU.add
                                        ).then_inc(dve_step, 1)

            def residue(s):
                dve.wait_ge(hi_done, s)
                nc.vector.tensor_tensor(t_b[:], sup_ps[:].rearrange("p (t f) -> p t f", f=F),
                                        support[:, bass.ds((s - 1) * TILES, TILES), 0:F], ALU.subtract
                                        ).then_inc(res_ready, 1)
                dve.wait_ge(part_done, s)
                dve.wait_ge(dve_step, base(s) + END_STEPS)
                own = x_all[:, bass.ds((s - 1) * TILES, TILES), :]
                nc.vector.tensor_tensor(own, own, tr_ps[:].rearrange("p (t f) -> p t f", f=F), ALU.add
                                        ).then_inc(own_done, 1)

            def sweep_block(s, b, first, start):
                end = start and not first
                for g in range(SLOTS):
                    if end and g == 2:
                        x1_sum(s)
                        x1_statistics(s)
                    masks(s, b, g, first, start)
                    if end and g == 0:
                        fold(s)
                    if end and g == 2:
                        h1_part(s)
                    row_sums(s, b, g, first, start)
                    if end and g == 3:
                        residue(s)

            piece_statistics(0)
            piece_h(0)
            masks(0, 0, 0, True, True)
            piece_statistics(1)
            masks(0, 0, 1, True, True)
            piece_h(1)
            piece_statistics(2)
            masks(0, 0, 2, True, True)
            piece_variance(2)
            piece_h(2)
            masks(0, 0, 3, True, True)
            piece_statistics(3)
            row_sums(0, 0, 2, True, True)
            piece_variance(3)
            masks(0, 1, 0, True, False)
            piece_h(3)
            row_sums(0, 0, 3, True, True)
            masks(0, 1, 1, True, False)
            piece_statistics(4)
            row_sums(0, 1, 0, True, False)
            masks(0, 1, 2, True, False)
            piece_variance(4)
            row_sums(0, 1, 1, True, False)
            piece_h(4)
            masks(0, 1, 3, True, False)
            row_sums(0, 1, 2, True, False)
            row_sums(0, 1, 3, True, False)
            loop(dve, 2, blocks, lambda b: sweep_block(0, b, True, False))
            scale_weight(setup_done - 6)
            with dve.Fori(1, strips) as s:
                sweep_block(s, 0, False, True)
                loop(dve, 1, blocks, lambda b: sweep_block(s, b, False, False))
            fold(strips)

            end_late = {3: x1_sum, 5: x1_statistics, 7: h1_part, 12: residue}

            def sums_out(s, done):
                dve.wait_ge(l1_done, done)
                if s > 1:
                    dve.wait_ge(fin_ps, s - 1)
                nc.vector.tensor_copy(feat_o[1], rank_ps[1][:] if s % 2 else part_ps[:, CHUNK:STRIP]).then_inc(o_dve, 1)

            def result(s):
                dve.wait_ge(fin_ps, s)
                if s > 2:
                    dve.wait_ge(out_done[(s - 1) % 2], (s - 1) // 2 * 16)
                nc.vector.tensor_tensor(t_a[:] if s % 2 else t_c[:], agg_ps[:].rearrange("p (t f) -> p t f", f=F),
                                        x_all[:, bass.ds((s - 1) * TILES, TILES), :], ALU.add).then_inc(y_ready, 1)

            def decode(b, g, before, empty):
                m = (before + b) * SLOTS + g
                dve.wait_ge(code_in[g], (before + b + 1) * 16)
                if not empty:
                    dve.wait_ge(l1_done, m - SLOTS + 1)
                cols = slice(0, GROUP * STRIP if empty else DVE_SHARE)
                nc.vector.tensor_scalar(adj[:, g, 2 * STRIP:4 * STRIP].bitcast(I16)[:, cols],
                                        adj[:, g, 0:STRIP].bitcast(U8)[:, cols], CODE_UNIT, None, ALU.mult
                                        ).then_inc(dec_dve, 1)

            for m in range(groups):
                decode(m // SLOTS, m % SLOTS, 0, m < SLOTS)
                if m in end_late:
                    end_late[m](strips)
            dve.wait_ge(own_done, strips)
            for s in range(1, strips):
                before = stored_before[s]
                for g in range(SLOTS):
                    decode(0, g, before, False)
                    if g == SUMS_AT:
                        sums_out(s, before * SLOTS)
                if stored_in[s] > 1:
                    decode(1, 0, before, False)
                    decode(1, 1, before, False)
                    result(s)
                    decode(1, 2, before, False)
                    decode(1, 3, before, False)
                    loop(dve, 2, stored_in[s], lambda b: [decode(b, g, before, False) for g in range(SLOTS)])
                else:
                    result(s)
            sums_out(strips, stored_total * SLOTS)
            result(strips)


def kernel(x, adj, L0_gnn_W, L1_gnn_weight, L1_gnn_bias):
    import numpy as np
    import concourse.bacc as bacc
    from concourse.bass_utils import run_bass_kernel_spmd

    x, adj = np.asarray(x), np.asarray(adj)
    n = x.shape[0]
    strips, tiles = n // STRIP, n // P
    adj_t = adj.reshape(strips, STRIP, tiles // GROUP, GROUP, P)[:, :, ::-1, ::-1, :]
    arrays = {
        "x_t": np.ascontiguousarray(x.reshape(tiles, P, F).transpose(1, 0, 2)),
        "adj_t": np.ascontiguousarray(adj_t.transpose(0, 2, 4, 3, 1)).reshape(strips, tiles // GROUP, P, GROUP * STRIP),
        "w_t": np.ascontiguousarray(np.asarray(L0_gnn_W).T),
        "weight": np.ascontiguousarray(L1_gnn_weight),
        "bias": np.ascontiguousarray(L1_gnn_bias),
    }
    nc = bacc.Bacc("TRN2", target_bir_lowering=False, num_devices=1)
    args = [nc.dram_tensor(k, a.shape, mybir.dt.from_np(a.dtype), kind="ExternalInput").ap() for k, a in arrays.items()]
    args.append(nc.dram_tensor("out_t", (P, tiles, F), F32, kind="ExternalOutput").ap())
    build_program(nc, *args)
    result = run_bass_kernel_spmd(nc, [arrays], core_ids=[0])
    return np.ascontiguousarray(result.results[0]["out_t"].transpose(1, 0, 2)).reshape(n, F)
```
